# Optimizing a Trainium2 kernel written in Bass

```python
import numpy as np
import jax
import jax.numpy as jnp

def _softmax(x, axis=-1):
    return jax.nn.softmax(x, axis=axis)

def _gelu(x):
    return jax.nn.gelu(x, approximate=True)

def _silu(x):
    return jax.nn.silu(x)

def _sigmoid(x):
    return jax.nn.sigmoid(x)

def _layernorm(x, axis=-1, eps=1e-05):
    m = jnp.mean(x, axis=axis, keepdims=True)
    v = jnp.var(x, axis=axis, keepdims=True)
    return (x - m) / jnp.sqrt(v + eps)

def _scatter_add(tgt, idx, src, axis=0):
    return tgt.at[idx].add(src)

def _segment_sum(src, seg, n):
    return jax.ops.segment_sum(src, seg, n)
kernel_name = 'mk_adaln_ffn_d1_seqx_r2_fd73b5'

def setup_inputs(seed: int=0):
    np.random.seed(seed)
    _w = jnp.asarray

    def _rec_inputs():
        import jax
        import jax.numpy as jnp
        _rk = jax.random.key(seed)
        x = -7.109e-05 + 0.9999 * jax.random.normal(jax.random.fold_in(_rk, 1), (32, 128, 1024), jnp.float32)
        _lenS = 128 - jax.random.randint(jax.random.fold_in(_rk, 7), (32,), 0, max(1, 128 // 4) + 1, jnp.int32)
        _lenS2 = 128 - jax.random.randint(jax.random.fold_in(_rk, 8), (32,), 0, max(1, 128 // 4) + 1, jnp.int32)
        itok_B_0_6 = jax.random.randint(jax.random.fold_in(_rk, 11), (32,), 0, 7, jnp.int32)
        return (x, itok_B_0_6)
    x, itok_B_0_6 = _rec_inputs()

    def _L0_cond_setup():
        import jax, jax.numpy as jnp
        import numpy as np
        B, T, D_IN, D_OUT = (16, 1024, 1024, 1024)
        N_ADAPTERS, RANK = (8, 16)
        key = jax.random.key(seed)
        k_x, k_w, k_a, k_b, k_s, k_idx = jax.random.split(key, 6)
        x = jax.random.normal(k_x, (B, T, D_IN), dtype=jnp.float32)
        W = jax.random.normal(k_w, (D_OUT, D_IN), dtype=jnp.float32) * (1.0 / np.sqrt(D_IN))
        A = jax.random.normal(k_a, (N_ADAPTERS, RANK, D_IN), dtype=jnp.float32) * 0.02
        Bm = jax.random.normal(k_b, (N_ADAPTERS, D_OUT, RANK), dtype=jnp.float32) * 0.02
        scalings = jnp.ones((N_ADAPTERS,), dtype=jnp.float32)
        adapter_idx = jax.random.randint(k_idx, (B,), 0, N_ADAPTERS, dtype=jnp.int32)
        return {'x': x, 'W': W, 'A': A, 'Bm': Bm, 'scalings': scalings, 'adapter_idx': adapter_idx}
    _L0_cond_all = _L0_cond_setup()
    _L0_cond_in = {k: v for k, v in _L0_cond_all.items() if k in ('W', 'A', 'Bm', 'scalings')}
    del _L0_cond_all

    def _L0_ffn_setup():
        import jax, jax.numpy as jnp
        import numpy as np
        FP8_MAX = 448.0
        SCALE_MARGIN = 0.8

        def _fp8_quant_dequant(t, scale):
            q = (t / scale).astype(jnp.float8_e4m3fn)
            return q.astype(jnp.float32) * scale
        key = jax.random.key(seed)
        k1, k2 = jax.random.split(key)
        B, S, D_IN, D_OUT = (4, 1024, 1024, 1024)
        x = jax.random.normal(k1, (B, S, D_IN), dtype=jnp.float32)
        weight = jax.random.normal(k2, (D_OUT, D_IN), dtype=jnp.float32)
        bias = jnp.zeros((D_OUT,), dtype=jnp.float32)
        return {'x': x, 'weight': weight, 'bias': bias}
    _L0_ffn_all = _L0_ffn_setup()
    _L0_ffn_in = {k: v for k, v in _L0_ffn_all.items() if k in ('weight', 'bias')}
    del _L0_ffn_all
    return {'x': x, 'itok_B_0_6': itok_B_0_6, 'L0_cond_W': _L0_cond_in['W'], 'L0_cond_A': _L0_cond_in['A'], 'L0_cond_Bm': _L0_cond_in['Bm'], 'L0_cond_scalings': _L0_cond_in['scalings'], 'L0_ffn_weight': _L0_ffn_in['weight'], 'L0_ffn_bias': _L0_ffn_in['bias']}

def reference(x, itok_B_0_6, L0_cond_W, L0_cond_A, L0_cond_Bm, L0_cond_scalings, L0_ffn_weight, L0_ffn_bias):
    import jax
    import jax.numpy as jnp

    def _L0_cond_ref(x, W, A, Bm, scalings, adapter_idx):
        import jax, jax.numpy as jnp
        import numpy as np
        B, T, D_IN, D_OUT = (16, 1024, 1024, 1024)
        N_ADAPTERS, RANK = (8, 16)
        H = jnp.einsum('btd,od->bto', x, W)
        A_b = A[adapter_idx]
        B_b = Bm[adapter_idx]
        s_b = scalings[adapter_idx]
        xa = jnp.einsum('btd,brd->btr', x, A_b)
        delta = jnp.einsum('btr,bor->bto', xa, B_b)
        delta = jax.lax.stop_gradient(delta * s_b[:, None, None])
        return H + delta

    def _L0_ffn_ref(x, weight, bias):
        import jax, jax.numpy as jnp
        import numpy as np
        FP8_MAX = 448.0
        SCALE_MARGIN = 0.8

        def _fp8_quant_dequant(t, scale):
            q = (t / scale).astype(jnp.float8_e4m3fn)
            return q.astype(jnp.float32) * scale
        amax_x = jnp.max(jnp.abs(x))
        amax_w = jnp.max(jnp.abs(weight))
        x_scale = amax_x / (FP8_MAX * SCALE_MARGIN)
        w_scale = jnp.maximum(amax_x, amax_w) / (FP8_MAX * SCALE_MARGIN)
        x_scale = jax.lax.stop_gradient(x_scale)
        w_scale = jax.lax.stop_gradient(w_scale)
        x_dq = _fp8_quant_dequant(x, x_scale)
        w_dq = _fp8_quant_dequant(weight, w_scale)
        out = jnp.einsum('bsd,od->bso', x_dq, w_dq)
        return out + bias
    x = x + _L0_ffn_ref(_L0_cond_ref(x, L0_cond_W, L0_cond_A, L0_cond_Bm, L0_cond_scalings, itok_B_0_6), L0_ffn_weight, L0_ffn_bias)
    return x

_drawn_inputs = setup_inputs


def setup_inputs(seed=0):
    import zlib

    import numpy as np

    out = dict(_drawn_inputs(seed))
    spreads = {'L0_cond_scalings': (1.0, 0.6), 'L0_ffn_bias': (0.0, 2.0)}
    factors = {}
    for name, (base, spread) in spreads.items():
        noise = np.random.default_rng([zlib.crc32(name.encode()), seed]).standard_normal(out[name].shape)
        drawn = base * np.exp(spread * noise) if base else spread * noise
        out[name] = jnp.asarray(drawn.astype(out[name].dtype))
    for name, factor in factors.items():
        out[name] = (out[name] * factor).astype(out[name].dtype)
    return out
```

```python
import concourse.bass as bass
from concourse import mybir

P = 128
N = 512
CHUNKS = 8
D = 1024
KT = D // P
BATCH = 32
SEQ = 128
PER_CHUNK = N // SEQ
SLOTS = 5
SPILLED = CHUNKS - SLOTS
LANDING = 4
BANKS = 8
FIRST_CREDIT = BANKS
STAGE1 = FIRST_CREDIT + CHUNKS * KT
FP8_RANGE = 448.0 * 0.8
TO_MAGIC = 2.0 ** 20
MAGIC_FLOOR = 1.5 * 2.0 ** 14
FIRST = 2 * KT
ORDER = list(range(SLOTS, CHUNKS)) + list(range(SPILLED, SLOTS)) + list(range(SPILLED))


def piece(i, half):
    return FIRST + 2 * (i - 1) + half


def adaln_ffn(nc, x, idx, W, A, B, scalings, adapter_of_row, ident, weight, bias, out):
    f32, f32r, bf16, i32 = mybir.dt.float32, mybir.dt.float32r, mybir.dt.bfloat16, mybir.dt.int32
    ALU, ACT, AX = mybir.AluOpType, mybir.ActivationFunctionType, mybir.AxisListType

    spill = nc.dram_tensor("spill", (SPILLED, P, KT, N), f32, kind="Internal").ap()

    KiB = 1024
    base = (nc.sbuf_base + 63) // 64 * 64

    def at(name, kib, shape, dt):
        return nc.alloc_sbuf_tensor_at(name, shape, dt, offset=base + int(kib * KiB))

    W_PLACE = [0, 1, 2, 3, 6, 7, 4, 5]
    w_parts = [at(f"w_parts_{t}", 8 * W_PLACE[t], [P, 2, KT, P], f32r) for t in range(KT)]
    h_all = at("h_all", 48, [P, SLOTS + 1, KT, N], f32)
    x_hi = at("x_hi", 144, [P, KT, N], f32r)
    x_lo = at("x_lo", 160, [P, KT, N], f32r)
    a_parts = at("a_parts", 176, [P, 2, KT, P], f32r)
    b_parts = at("b_parts", 184, [P, 2, D], f32r)
    x_land = at("x_land", 192, [P, LANDING, N], f32)
    xa = at("xa", 200, [P, N], f32)
    xa_hi = at("xa_hi", 202, [P, N], f32r)
    xa_lo = at("xa_lo", 204, [P, N], f32r)
    a_land = at("a_land", 64, [P, KT, P], f32)
    b_land = at("b_land", 68, [P, D], f32)
    weight_early = at("weight_early", 80, [P, KT, D], f32)
    w_land = at("w_land", 112, [P, KT, KT, P], f32)
    weight_f = at("weight_f", 0, [P, KT, D], f32)
    q = at("q", 32, [P, 2, KT, N], bf16)
    o = at("o", 144, [P, 2, KT, N], f32)
    weight_q = at("weight_q", 176, [P, KT, D], bf16)
    magic = at("magic", 192, [P, 2, 4 * N], bf16)
    SMALL = 206
    idx_i = at("idx_i", SMALL, [P, BATCH], i32)
    mask = at("mask", SMALL + 0.125, [P, BATCH], f32)
    scal = at("scal", SMALL + 0.25, [P, 2], f32)
    maxima = at("maxima", SMALL + 0.3125, [P, CHUNKS * KT], f32)
    peak = at("peak", SMALL + 0.5625, [P, 2], f32)
    peak_row = at("peak_row", SMALL + 0.59375, [1, 2], f32)
    scale = at("scale", SMALL + 0.625, [P, 2], f32)
    inv = at("inv", SMALL + 0.65625, [P, 2], f32)
    inv_magic = at("inv_magic", SMALL + 0.6875, [P, 2], f32)
    rescale = at("rescale", SMALL + 0.71875, [P, 1], f32)
    bias_sb = at("bias_sb", SMALL + 0.75, [P, KT], f32)
    ones = at("ones", SMALL + 0.8125, [1, P], f32)
    ident_sb = at("ident_sb", SMALL + 1.3125, [P, P], f32)

    bank = [nc.alloc_psum_tensor(f"bank_{i}", [P, N], f32) for i in range(BANKS)]
    XA_BANK = BANKS - 1

    def bank_of(t):
        return bank[t % (BANKS - 1)]

    sem = nc.alloc_semaphore
    a_landed, b_landed, small_landed = sem("a_landed"), sem("b_landed"), sem("small_landed")
    w_landed = [sem(f"w_landed_{t}") for t in range(KT)]
    weight_early_landed, weight_landed = sem("weight_early_landed"), sem("weight_landed")
    x_landed = [sem(f"x_landed_{r}") for r in range(LANDING)]
    a_hi_ready, a_lo_ready = sem("a_hi_ready"), sem("a_lo_ready")
    b_hi_ready, b_lo_ready = sem("b_hi_ready"), sem("b_lo_ready")
    w_hi_ready, w_lo_ready = sem("w_hi_ready"), sem("w_lo_ready")
    x_hi_ready, x_lo_ready, x_used = sem("x_hi_ready"), sem("x_lo_ready"), sem("x_used")
    ids_ready, mask_ready, weight_peak_ready = sem("ids_ready"), sem("mask_ready"), sem("weight_peak_ready")
    ax_done, xa_ready, xa_hi_ready, xa_lo_ready = sem("ax_done"), sem("xa_ready"), sem("xa_hi_ready"), sem("xa_lo_ready")
    tile_done, banks_free, maxima_ready = sem("tile_done"), sem("banks_free"), sem("maxima_ready")
    spilled = sem("spilled")
    ones_ready, peak_ready, peaks_turned, peak_row_ready = (
        sem("ones_ready"), sem("peak_ready"), sem("peaks_turned"), sem("peak_row_ready"))
    peaks_spread, dve_step, scales_ready = sem("peaks_spread"), sem("dve_step"), sem("scales_ready")
    reloaded = [sem(f"reloaded_{c}") for c in range(SPILLED)]
    magic_raw, magic_ready, sum_ready, quantised = (
        sem("magic_raw"), sem("magic_ready"), sem("sum_ready"), sem("quantised"))
    tile2_done = sem("tile2_done")
    x_added = [[sem(f"x_added_{b}{half}") for half in range(2)] for b in range(2)]
    o_free = [[sem(f"o_free_{b}{half}") for half in range(2)] for b in range(2)]

    def slot(s):
        return s + 1

    def stage2_slot(i):
        return i + 1 if i < SLOTS else i - SLOTS

    with nc.Block() as block:

        @block.sync
        def _(sp):
            sp.dma_start(a_land[:, :, :], A).then_inc(a_landed, 16)

            def load_x(c, k):
                sp.dma_start(x_land[:, k % LANDING, :], x[c, :, k, :]).then_inc(x_landed[k % LANDING], 16)

            for k in range(LANDING):
                load_x(0, k)
            sp.dma_start(w_land[:, 0, :, :], W[:, 0, :, :]).then_inc(w_landed[0], 16)
            sp.dma_start(idx_i[:, :], idx).then_inc(small_landed, 16)
            sp.dma_start(scal[:, 0:1], scalings).then_inc(small_landed, 16)
            sp.dma_start(scal[:, 1:2], adapter_of_row).then_inc(small_landed, 16)
            sp.dma_start(b_land[:, :], B).then_inc(b_landed, 16)
            for k in range(LANDING, KT):
                sp.wait_ge(x_lo_ready, k - LANDING + 1)
                load_x(0, k)
            for t in range(1, KT):
                sp.dma_start(w_land[:, t, :, :], W[:, t, :, :]).then_inc(w_landed[t], 16)
            sp.dma_start(weight_early[:, :, :], weight).then_inc(weight_early_landed, 16)
            sp.dma_start(ident_sb[:, :], ident).then_inc(small_landed, 16)
            sp.dma_start(bias_sb[:, :], bias).then_inc(small_landed, 16)
            with sp.Fori(1, CHUNKS) as c:
                for k in range(KT):
                    sp.wait_ge(x_lo_ready, c * KT + k - LANDING + 1)
                    load_x(c, k)
            sp.wait_ge(tile_done, (CHUNKS - 1) * KT + 4)
            sp.dma_start(weight_f[:, :, :], weight).then_inc(weight_landed, 16)
            sp.wait_ge(spilled, 16 * SPILLED)
            sp.wait_ge(tile_done, (CHUNKS - 1) * KT + 6)
            sp.dma_start(h_all[:, 0, :, :], spill[0]).then_inc(reloaded[0], 16)
            for i in (1, 2):
                sp.wait_ge(quantised, FIRST if i == 1 else piece(1, 1) + 1)
                sp.dma_start(h_all[:, slot(i - 1), :, :], spill[i]).then_inc(reloaded[i], 16)

            def store(m, b, i):
                for half in range(2):
                    ts = slice(half * KT // 2, (half + 1) * KT // 2)
                    sp.wait_ge(x_added[b][half], 16 * (m + 1))
                    sp.dma_start(out[i, :, ts, :], o[:, b, ts, :]).then_inc(o_free[b][half], 16)

            with sp.Fori(0, CHUNKS // 2) as m:
                for b in range(2):
                    store(m, b, 2 * m + b)
            for b in range(2):
                for half in range(2):
                    sp.wait_ge(o_free[b][half], 16 * (CHUNKS // 2 + 1))

        @block.gpsimd
        def _(pool):
            nc.gpsimd.memset(ones[:, :], 1.0).then_inc(ones_ready, 1)
            with pool.Fori(0, SPILLED) as c:
                pool.wait_ge(banks_free, FIRST_CREDIT + (c + 1) * KT)
                pool.dma_start(spill[c], h_all[:, c + 1, :, :], max_dma_last_dim=16384).then_inc(spilled, 16)
                pool.wait_ge(spilled, 16 * (c + 1))
            for i in range(CHUNKS):
                b = i % 2
                for half in range(2):
                    ts = slice(half * KT // 2, (half + 1) * KT // 2)
                    pool.wait_ge(banks_free, STAGE1 + i * KT + (half + 1) * KT // 2)
                    pool.dma_start(o[:, b, ts, :], x[ORDER[i], :, ts, :], accum_op=ALU.add,
                                   max_dma_last_dim=8192).then_inc(x_added[b][half], 16)

        @block.tensor
        def _(pe):
            def three(ps, hi, lo, mov_hi, mov_lo, start, stop):
                nc.tensor.matmul(ps, lo, mov_hi, start=start, stop=False)
                nc.tensor.matmul(ps, hi, mov_lo, start=False, stop=False)
                return nc.tensor.matmul(ps, hi, mov_hi, start=False, stop=stop)

            pe.wait_ge(a_lo_ready, 1)
            with pe.Fori(0, CHUNKS) as c:
                for k in range(KT):
                    pe.wait_ge(x_lo_ready, c * KT + k + 1)
                    last = three(bank[XA_BANK][:, :], a_parts[:, 0, k, :], a_parts[:, 1, k, :],
                                 x_hi[:, k, :], x_lo[:, k, :], k == 0, k == KT - 1)
                last.then_inc(ax_done, 1)
                for t in range(KT):
                    pe.wait_ge(w_lo_ready, t + 1)
                    pe.wait_ge(banks_free, c * KT + (FIRST_CREDIT + 1 if t == KT - 1 else KT if t == 0 else t + 1))
                    for k in range(KT):
                        last = three(bank_of(t)[:, :], w_parts[t][:, 0, k, :], w_parts[t][:, 1, k, :],
                                     x_hi[:, k, :], x_lo[:, k, :], k == 0, False)
                        if t == KT - 1:
                            last.then_inc(x_used, 1)
                    if t == 0:
                        pe.wait_ge(b_lo_ready, 1)
                        pe.wait_ge(xa_lo_ready, c + 1)
                    os = slice(t * P, (t + 1) * P)
                    three(bank_of(t)[:, :], b_parts[:, 0, os], b_parts[:, 1, os],
                          xa_hi[:, :], xa_lo[:, :], False, True).then_inc(tile_done, 1)

            pe.wait_ge(small_landed, 16 * 5)
            pe.wait_ge(peak_ready, 1)
            for j in range(2):
                last = nc.tensor.matmul(bank[XA_BANK][0:1, j * P:(j + 1) * P], peak[:, j:j + 1], ident_sb[:, :],
                                        start=True, stop=True)
            last.then_inc(peaks_turned, 1)
            pe.wait_ge(ones_ready, 1)
            pe.wait_ge(peak_row_ready, 1)
            nc.tensor.matmul(bank[XA_BANK - 1][:, 0:2], ones[0:1, :], peak_row[0:1, :],
                             start=True, stop=True).then_inc(peaks_spread, 1)

            for k in range(KT):
                pe.wait_ge(quantised, 2 * k + 2)
                for t in range(KT):
                    last = nc.tensor.matmul(bank[t][:, :], weight_q[:, k, t * P:(t + 1) * P], q[:, 0, k, :],
                                            start=k == 0, stop=k == KT - 1)
                    if k == KT - 1:
                        last.then_inc(tile2_done, 1)

            def chunk(i, b):
                for t in range(KT):
                    pe.wait_ge(banks_free, STAGE1 + (i - 1) * KT + t + 1)
                    for k in range(KT):
                        if t == 0 and k % (KT // 2) == 0:
                            pe.wait_ge(quantised, piece(i, k // (KT // 2)) + 1)
                        last = nc.tensor.matmul(bank[t][:, :], weight_q[:, k, t * P:(t + 1) * P], q[:, b, k, :],
                                                start=k == 0, stop=k == KT - 1)
                    last.then_inc(tile2_done, 1)

            chunk(1, 1)
            with pe.Fori(1, CHUNKS // 2) as m:
                chunk(2 * m, 0)
                chunk(2 * m + 1, 1)

        @block.scalar
        def _(act):
            def split_x(c, k):
                act.wait_ge(x_landed[k % LANDING], 16 * (2 * c + k // LANDING + 1))
                nc.scalar.activation(x_hi[:, k, :], x_land[:, k % LANDING, :], ACT.Copy).then_inc(x_hi_ready, 1)

            def split_w(t):
                act.wait_ge(w_landed[t], 16)
                nc.scalar.activation(w_parts[t][:, 0, :, :], w_land[:, t, :, :], ACT.Copy).then_inc(w_hi_ready, 1)

            def chunk(c, s, first=False, last=False):
                act.wait_ge(ax_done, c + 1)
                for j in range(PER_CHUNK):
                    ns = slice(j * SEQ, (j + 1) * SEQ)
                    done = nc.scalar.activation(xa[:, ns], bank[XA_BANK][:, ns], ACT.Copy,
                                                scale=mask[:, bass.ds(c * PER_CHUNK + j, 1)])
                done.then_inc(xa_ready, 1)
                act.wait_ge(xa_ready, c + 1)
                nc.scalar.activation(xa_hi[:, :], xa[:, :], ACT.Copy).then_inc(xa_hi_ready, 1)
                for t in range(KT):
                    if first and t + 2 < KT:
                        split_w(t + 2)
                    if not last and t == KT - 1:
                        for k in range(KT):
                            act.wait_ge(x_used, c * KT + k + 1)
                            split_x(c + 1, k)
                    act.wait_ge(tile_done, c * KT + t + 1)
                    nc.scalar.activation(h_all[:, s, t, :], bank_of(t)[:, :], ACT.Copy).then_inc(banks_free, 1)

            act.wait_ge(a_landed, 16)
            nc.scalar.activation(a_parts[:, 0, :, :], a_land[:, :, :], ACT.Copy).then_inc(a_hi_ready, 1)
            for k in range(KT):
                split_x(0, k)
            split_w(0)
            act.wait_ge(b_landed, 16)
            nc.scalar.activation(b_parts[:, 0, :], b_land[:, :], ACT.Copy).then_inc(b_hi_ready, 1)
            split_w(1)
            act.wait_ge(b_hi_ready, 1)
            act.sem_inc(banks_free, FIRST_CREDIT)
            for b in range(2):
                for half in range(2):
                    act.sem_inc(o_free[b][half], 16)
            act.wait_ge(mask_ready, 1)
            act.wait_ge(b_lo_ready, 1)
            chunk(0, slot(0), first=True)
            act.wait_ge(weight_peak_ready, 1)
            act.wait_ge(w_lo_ready, KT)
            with act.Fori(1, SLOTS) as c:
                chunk(c, c + 1)
            with act.Fori(SLOTS, CHUNKS - 1) as c:
                act.wait_ge(spilled, 16 * (c - SLOTS + 1))
                chunk(c, c - SLOTS + 1)
            act.wait_ge(spilled, 16 * SPILLED)
            chunk(CHUNKS - 1, slot(CHUNKS - 1 - SLOTS), last=True)

            def magic_of(n, b, src, side, shape):
                if not isinstance(n, int) or n >= 2:
                    act.wait_ge(quantised, n - 1)
                nc.scalar.activation(shape(magic[:, b, :]), src, ACT.Abs,
                                     scale=inv_magic[:, side:side + 1]).then_inc(magic_raw, 1)

            def half_chunk(i, half, s):
                ks = slice(half * KT // 2, (half + 1) * KT // 2)
                magic_of(piece(i, half), half, h_all[:, s, ks, :], 0,
                         lambda ap: ap.rearrange("p (k n) -> p k n", n=N))

            def evacuate(i, m, b, half):
                act.wait_ge(o_free[b][half], 16 * (m + 1))
                for t in range(half * KT // 2, (half + 1) * KT // 2):
                    act.wait_ge(tile2_done, i * KT + t + 1)
                    nc.scalar.activation(o[:, b, t, :], bank[t][:, :], ACT.Identity, bias=bias_sb[:, t:t + 1],
                                         scale=rescale[:, 0:1]).then_inc(banks_free, 1)

            act.wait_ge(scales_ready, 1)
            act.wait_ge(weight_landed, 16)
            for k in range(KT):
                magic_of(2 * k, 0, h_all[:, slot(0), k, :], 0, lambda ap: ap[:, 0:N])
                magic_of(2 * k + 1, 1, weight_f[:, k, :], 1, lambda ap: ap[:, 0:D])
            half_chunk(1, 0, stage2_slot(1))
            act.wait_ge(reloaded[0], 16)
            with act.Fori(0, 2) as m:
                for b in range(2):
                    i = 2 * m + b
                    half_chunk(i + 1, 1, i + 2)
                    evacuate(i, m, b, 0)
                    if b == 0:
                        half_chunk(i + 2, 0, i + 3)
                    else:
                        half_chunk(i + 2, 0, (i + 3) % (SLOTS + 1))
                    evacuate(i, m, b, 1)
            for i in range(4, CHUNKS):
                if i + 1 < CHUNKS:
                    half_chunk(i + 1, 1, stage2_slot(i + 1))
                evacuate(i, i // 2, i % 2, 0)
                if i + 2 < CHUNKS:
                    act.wait_ge(reloaded[i + 2 - SLOTS], 16)
                    half_chunk(i + 2, 0, stage2_slot(i + 2))
                evacuate(i, i // 2, i % 2, 1)

        @block.vector
        def _(dve):
            steps = [0]

            def then(instruction):
                steps[0] += 1
                instruction.then_inc(dve_step, 1)
                dve.wait_ge(dve_step, steps[0])

            def split_x(c, k):
                dve.wait_ge(x_hi_ready, c * KT + k + 1)
                nc.vector.tensor_tensor(x_lo[:, k, :], x_land[:, k % LANDING, :], x_hi[:, k, :].bitcast(f32),
                                        ALU.subtract).then_inc(x_lo_ready, 1)

            def split_w(t):
                dve.wait_ge(w_hi_ready, t + 1)
                nc.vector.tensor_tensor(w_parts[t][:, 1, :, :], w_land[:, t, :, :],
                                        w_parts[t][:, 0, :, :].bitcast(f32), ALU.subtract).then_inc(w_lo_ready, 1)

            def split_xa(c):
                dve.wait_ge(xa_hi_ready, c + 1)
                nc.vector.tensor_tensor(xa_lo[:, :], xa[:, :], xa_hi[:, :].bitcast(f32),
                                        ALU.subtract).then_inc(xa_lo_ready, 1)

            def chunk(c, s, first=False, last=False):
                split_xa(c)
                for t in range(KT):
                    if first and t + 2 < KT:
                        split_w(t + 2)
                    if not last and t == KT - 1:
                        for k in range(KT):
                            split_x(c + 1, k)
                    dve.wait_ge(banks_free, FIRST_CREDIT + c * KT + t + 1)
                    nc.vector.tensor_reduce(maxima[:, bass.ds(c * KT + t, 1)], h_all[:, s, t, :], AX.X, ALU.max,
                                            apply_absolute_value=True).then_inc(maxima_ready, 1)

            dve.wait_ge(a_hi_ready, 1)
            nc.vector.tensor_tensor(a_parts[:, 1, :, :], a_land[:, :, :], a_parts[:, 0, :, :].bitcast(f32),
                                    ALU.subtract).then_inc(a_lo_ready, 1)
            for k in range(KT):
                split_x(0, k)
            split_w(0)
            dve.wait_ge(small_landed, 16 * 3)
            then(nc.vector.tensor_copy(mask[:, :], idx_i[:, :]))
            nc.vector.tensor_scalar(mask[:, :], mask[:, :], scal[:, 1:2], scal[:, 0:1],
                                    ALU.is_equal, ALU.mult).then_inc(mask_ready, 1)
            dve.wait_ge(b_hi_ready, 1)
            nc.vector.tensor_tensor(b_parts[:, 1, :], b_land[:, :], b_parts[:, 0, :].bitcast(f32),
                                    ALU.subtract).then_inc(b_lo_ready, 1)
            split_w(1)
            chunk(0, slot(0), first=True)
            dve.wait_ge(weight_early_landed, 16)
            nc.vector.tensor_reduce(peak[:, 1:2], weight_early[:, :, :], AX.XY, ALU.max,
                                    apply_absolute_value=True).then_inc(weight_peak_ready, 1)
            with dve.Fori(1, SLOTS) as c:
                chunk(c, c + 1)
            with dve.Fori(SLOTS, CHUNKS - 1) as c:
                chunk(c, c - SLOTS + 1)
            chunk(CHUNKS - 1, slot(CHUNKS - 1 - SLOTS), last=True)

            dve.wait_ge(maxima_ready, CHUNKS * KT)
            nc.vector.tensor_reduce(peak[:, 0:1], maxima[:, :], AX.X, ALU.max).then_inc(peak_ready, 1)
            dve.wait_ge(peaks_turned, 1)
            nc.vector.tensor_reduce(peak_row[0:1, :], bank[XA_BANK][0:1, 0:2 * P].rearrange("a (j p) -> a j p", j=2),
                                    AX.X, ALU.max).then_inc(peak_row_ready, 1)
            dve.wait_ge(peaks_spread, 1)
            then(nc.vector.tensor_copy(scale[:, :], bank[XA_BANK - 1][:, 0:2]))
            then(nc.vector.tensor_tensor(scale[:, 1:2], scale[:, 0:1], scale[:, 1:2], ALU.max))
            then(nc.vector.tensor_scalar(scale[:, :], scale[:, :], 1.0 / FP8_RANGE, None, ALU.mult))
            then(nc.vector.reciprocal(inv[:, :], scale[:, :]))
            nc.vector.tensor_tensor(rescale[:, :], scale[:, 0:1], scale[:, 1:2], ALU.mult)
            then(nc.vector.tensor_scalar(inv_magic[:, :], inv[:, :], TO_MAGIC, None, ALU.mult))
            dve.sem_inc(scales_ready, 1)

            def quantise(n, b, src, dst, side, shape):
                dve.wait_ge(magic_raw, n + 1)
                m = magic[:, b, :]
                nc.vector.tensor_scalar(shape(m), shape(m), MAGIC_FLOOR, None, ALU.max).then_inc(magic_ready, 1)
                dve.wait_ge(magic_ready, n + 1)
                nc.vector.scalar_tensor_tensor(src, src, inv[:, side:side + 1], shape(m),
                                               ALU.mult, ALU.add).then_inc(sum_ready, 1)
                dve.wait_ge(sum_ready, n + 1)
                nc.vector.tensor_tensor(dst, src, shape(m), ALU.subtract).then_inc(quantised, 1)

            def quantise_chunk(i, b, s):
                for half in range(2):
                    ks = slice(half * KT // 2, (half + 1) * KT // 2)
                    quantise(piece(i, half), half, h_all[:, s, ks, :], q[:, b, ks, :], 0,
                             lambda ap: ap.rearrange("p (k n) -> p k n", n=N))

            for k in range(KT):
                quantise(2 * k, 0, h_all[:, slot(0), k, :], q[:, 0, k, :], 0, lambda ap: ap[:, 0:N])
                quantise(2 * k + 1, 1, weight_f[:, k, :], weight_q[:, k, :], 1, lambda ap: ap[:, 0:D])
            quantise_chunk(1, 1, stage2_slot(1))
            with dve.Fori(2, SLOTS) as i:
                dve.wait_ge(tile2_done, (i - 1) * KT)
                quantise_chunk(i, i % 2, i + 1)
            with dve.Fori(SLOTS, CHUNKS) as i:
                dve.wait_ge(tile2_done, (i - 1) * KT)
                quantise_chunk(i, i % 2, i - SLOTS)


def kernel(x, itok_B_0_6, L0_cond_W, L0_cond_A, L0_cond_Bm, L0_cond_scalings, L0_ffn_weight, L0_ffn_bias):
    import numpy as np
    import concourse.bacc as bacc
    from concourse.bass_utils import run_bass_kernel_spmd

    def laid_out(a, *axes):
        return np.ascontiguousarray(np.transpose(a, axes))

    f = np.asarray
    rank = L0_cond_A.shape[1]
    arrays = {
        "x": laid_out(f(x).reshape(CHUNKS, N, KT, P), 0, 3, 2, 1),
        "idx": np.ascontiguousarray(np.broadcast_to(f(itok_B_0_6), (P, BATCH))),
        "W": laid_out(f(L0_cond_W).reshape(KT, P, KT, P), 3, 0, 2, 1),
        "A": laid_out(f(L0_cond_A).reshape(P, KT, P), 2, 1, 0),
        "B": laid_out(f(L0_cond_Bm), 0, 2, 1).reshape(P, D),
        "scalings": np.repeat(f(L0_cond_scalings), rank).reshape(P, 1),
        "adapter_of_row": (np.arange(P) // rank).astype(np.float32).reshape(P, 1),
        "ident": np.eye(P, dtype=np.float32),
        "weight": laid_out(f(L0_ffn_weight).reshape(D, KT, P), 2, 1, 0),
        "bias": laid_out(f(L0_ffn_bias).reshape(KT, P), 1, 0),
    }
    nc = bacc.Bacc("TRN2", target_bir_lowering=False, num_devices=1)
    args = [nc.dram_tensor(f"in_{name}", a.shape, mybir.dt.from_np(a.dtype), kind="ExternalInput").ap()
            for name, a in arrays.items()]
    out = nc.dram_tensor("out", (CHUNKS, P, KT, N), mybir.dt.float32, kind="ExternalOutput").ap()
    adaln_ffn(nc, *args, out)
    run = run_bass_kernel_spmd(nc, [{f"in_{name}": a for name, a in arrays.items()}], core_ids=[0])
    got = np.empty((CHUNKS, N, KT, P), np.float32)
    got[ORDER] = run.results[0]["out"].transpose(0, 3, 2, 1)
    return got.reshape(BATCH, SEQ, D)
```

```python
import concourse.bass as bass
from concourse import mybir

P = 128
N = 512
CHUNKS = 8
D = 1024
KT = D // P
BATCH = 32
ADAPTERS = 8
RANK = 16
ROWS = 2 * RANK
SEQ = 128
PER_CHUNK = N // SEQ
SLOTS = 5
SPILLED = CHUNKS - SLOTS
LANDING = 4
BANKS = 8
SPLIT_A = [2, 4]
FIRST_CREDIT = BANKS
STAGE1 = FIRST_CREDIT + CHUNKS * KT
FP8_RANGE = 448.0 * 0.8
TO_MAGIC = 2.0 ** 20
MAGIC_FLOOR = 1.5 * 2.0 ** 14
SCALED = 2 * KT
SMALL_MAGICS = 4
FIRST = 2 * KT
ORDER = list(range(SLOTS, CHUNKS)) + list(range(SPILLED, SLOTS)) + list(range(SPILLED))


def piece(i, half):
    return FIRST + 2 * (i - 1) + half


def quadrants(j):
    low = (j + 2) % 4
    return slice(j * ROWS, (j + 1) * ROWS), slice(low * ROWS, (low + 1) * ROWS)


def adaln_ffn(nc, x, idx, W, A, B, scalings, ident, weight, bias, out):
    f32, f32r, bf16, i32 = mybir.dt.float32, mybir.dt.float32r, mybir.dt.bfloat16, mybir.dt.int32
    ALU, ACT, AX = mybir.AluOpType, mybir.ActivationFunctionType, mybir.AxisListType

    spill = nc.dram_tensor("spill", (SPILLED, P, KT, N), f32, kind="Internal").ap()
    b_table = nc.dram_tensor("b_table", (ADAPTERS, 2, RANK, D), f32, kind="Internal").ap()

    KiB = 1024
    base = (nc.sbuf_base + 63) // 64 * 64

    def at(name, kib, shape, dt):
        return nc.alloc_sbuf_tensor_at(name, shape, dt, offset=base + int(kib * KiB))

    W_PLACE = [0, 1, 2, 3, 6, 7, 4, 5]
    w_parts = [at(f"w_parts_{t}", 8 * W_PLACE[t], [P, 2, KT, P], f32r) for t in range(KT)]
    h_all = at("h_all", 48, [P, SLOTS + 1, KT, N], f32)
    x_hi = at("x_hi", 144, [P, KT, N], f32r)
    x_lo = at("x_lo", 160, [P, KT, N], f32r)
    a_all = at("a_all", 176, [P, KT, ADAPTERS, RANK], f32)
    a_parts = at("a_parts", 180, [P, 2, KT, PER_CHUNK, 2, RANK], f32r)
    b_parts = at("b_parts", 188, [P, 2, D], f32r)
    xa = at("xa", 196, [P, 2, 2 * SEQ], f32r)
    x_land = at("x_land", 198, [P, LANDING, N], f32)
    b_land = at("b_land", 64, [P, D], f32)
    b_hi = at("b_hi", 68, [P, D], f32)
    b_lo = at("b_lo", 72, [P, D], f32)
    a_first = [at(f"a_first_{pair}", 76 + pair, [P, KT, 2, RANK], f32) for pair in range(2)]
    weight_early = at("weight_early", 80, [P, KT, D], f32)
    w_land = at("w_land", 112, [P, KT, KT, P], f32)
    weight_f = at("weight_f", 0, [P, KT, D], f32)
    q = at("q", 32, [P, 2, KT, N], bf16)
    o = at("o", 144, [P, 2, KT, N], f32)
    weight_q = at("weight_q", 176, [P, KT, D], bf16)
    magic = at("magic", 192, [P, KT, N], bf16)
    ident_sb = at("ident_sb", 200, [P, P], f32)
    ones = at("ones", 201, [1, P], f32)
    x_last = at("x_last", 0, [P, KT, N], f32)
    SMALL = 206
    idx_i = at("idx_i", SMALL, [P, BATCH], i32)
    s_batch = at("s_batch", SMALL + 0.125, [P, BATCH], f32)
    s_adapter = at("s_adapter", SMALL + 0.25, [P, ADAPTERS], f32)
    weight_maxima = at("weight_maxima", SMALL + 0.28125, [P, KT], f32)
    maxima = at("maxima", SMALL + 0.3125, [P, CHUNKS * KT], f32)
    peak = at("peak", SMALL + 0.5625, [P, 2], f32)
    peak_row = at("peak_row", SMALL + 0.59375, [1, 2], f32)
    scale = at("scale", SMALL + 0.625, [P, 2], f32)
    inv = at("inv", SMALL + 0.65625, [P, 2], f32)
    inv_magic = at("inv_magic", SMALL + 0.6875, [P, 2], f32)
    rescale = at("rescale", SMALL + 0.71875, [P, 1], f32)
    bias_sb = at("bias_sb", SMALL + 0.75, [P, KT], f32)
    a_now = at("a_now", SMALL + 0.8125, [P, KT, 2, RANK], f32)

    bank = [nc.alloc_psum_tensor(f"bank_{i}", [P, N], f32) for i in range(BANKS)]
    XA_BANK = BANKS - 1

    sem = nc.alloc_semaphore
    a_landed, b_landed, small_landed, scalings_landed = (
        sem("a_landed"), sem("b_landed"), sem("small_landed"), sem("scalings_landed"))
    w_landed = [sem(f"w_landed_{t}") for t in range(KT)]
    weight_early_landed, weight_landed = sem("weight_early_landed"), sem("weight_landed")
    x_landed = [sem(f"x_landed_{r}") for r in range(LANDING)]
    a_now_ready, a_hi_ready, a_lo_ready = sem("a_now_ready"), sem("a_hi_ready"), sem("a_lo_ready")
    b_hi_ready, b_lo_ready = sem("b_hi_ready"), sem("b_lo_ready")
    b_table_ready, b_gathered, xa_zeroed = sem("b_table_ready"), sem("b_gathered"), sem("xa_zeroed")
    idx_landed = sem("idx_landed")
    w_hi_ready, w_lo_ready = sem("w_hi_ready"), sem("w_lo_ready")
    x_hi_ready, x_lo_ready, x_used = sem("x_hi_ready"), sem("x_lo_ready"), sem("x_used")
    weight_maxima_ready = sem("weight_maxima_ready")
    ax_done, xa_hi_ready, xa_lo_ready = sem("ax_done"), sem("xa_hi_ready"), sem("xa_lo_ready")
    x_last_landed, x_last_ready, last_out_ready, last_stored = (
        sem("x_last_landed"), sem("x_last_ready"), sem("last_out_ready"), sem("last_stored"))
    tile_done, banks_free, maxima_ready = sem("tile_done"), sem("banks_free"), sem("maxima_ready")
    spilled = sem("spilled")
    ones_ready, peak_ready, peaks_turned, peak_row_ready = (
        sem("ones_ready"), sem("peak_ready"), sem("peaks_turned"), sem("peak_row_ready"))
    peaks_spread, dve_step, scales_ready, rescale_ready = (
        sem("peaks_spread"), sem("dve_step"), sem("scales_ready"), sem("rescale_ready"))
    reloaded = [sem(f"reloaded_{c}") for c in range(SPILLED)]
    magic_raw, magic_ready, sum_ready, quantised = (
        sem("magic_raw"), sem("magic_ready"), sem("sum_ready"), sem("quantised"))
    tile2_done = sem("tile2_done")
    x_added = [[sem(f"x_added_{b}{half}") for half in range(2)] for b in range(2)]
    o_free = [[sem(f"o_free_{b}{half}") for half in range(2)] for b in range(2)]

    def slot(s):
        return s + 1

    def stage2_slot(i):
        return i + 1 if i < SLOTS else i - SLOTS

    def half_magic(half):
        return magic[:, half * 4:(half + 1) * 4, :]

    def small_magic(n):
        b = n % SMALL_MAGICS
        return magic[:, 2 * b, :] if n % 2 == 0 else magic[:, 2 * b:2 * b + 2, :].rearrange("p a n -> p (a n)")

    with nc.Block() as block:

        @block.sync
        def _(sp):
            def load_x(c, k):
                sp.dma_start(x_land[:, k % LANDING, :], x[c, :, k, :]).then_inc(x_landed[k % LANDING], 16)

            def gather_b(c):
                for j in range(PER_CHUNK):
                    n = sp.value_load(idx_i[0:1, bass.ds(c * PER_CHUNK + j, 1)], min_val=0, max_val=ADAPTERS - 1)
                    for rows in quadrants(j):
                        sp.dma_start(b_parts[rows, j // 2, :].bitcast(f32),
                                     b_table[n, :, :, :].rearrange("part r o -> (part r) o")
                                     ).then_inc(b_gathered, 16)

            load_x(0, 0)
            sp.dma_start(w_land[:, 0, :, :], W[:, 0, :, :]).then_inc(w_landed[0], 16)
            sp.dma_start(idx_i[:, :], idx).then_inc(idx_landed, 16)
            for k in range(1, LANDING):
                load_x(0, k)
            sp.dma_start(s_adapter[:, :], scalings).then_inc(scalings_landed, 16)
            sp.dma_start(a_all[:, :, :, :], A).then_inc(a_landed, 16)
            sp.dma_start(b_land[:, :], B).then_inc(b_landed, 16)
            for k in range(LANDING, KT):
                sp.wait_ge(x_lo_ready, k - LANDING + 1)
                load_x(0, k)
            sp.dma_start(w_land[:, 1, :, :], W[:, 1, :, :]).then_inc(w_landed[1], 16)
            sp.wait_ge(b_hi_ready, 1)
            sp.dma_start(b_table[:, 0, :, :], b_hi[:, :]).then_inc(b_table_ready, 16)
            sp.wait_ge(b_lo_ready, 1)
            sp.dma_start(b_table[:, 1, :, :], b_lo[:, :]).then_inc(b_table_ready, 16)
            sp.wait_ge(b_table_ready, 32)
            gather_b(0)
            for t in range(2, KT):
                sp.dma_start(w_land[:, t, :, :], W[:, t, :, :]).then_inc(w_landed[t], 16)
            sp.dma_start(weight_early[:, :, :], weight).then_inc(weight_early_landed, 16)
            sp.dma_start(bias_sb[:, :], bias).then_inc(small_landed, 16)
            with sp.Fori(1, CHUNKS) as c:
                for k in range(KT):
                    sp.wait_ge(x_lo_ready, c * KT + k - LANDING + 1)
                    load_x(c, k)
                sp.wait_ge(tile_done, c * KT)
                gather_b(c)
            sp.wait_ge(x_lo_ready, CHUNKS * KT)
            sp.dma_start(ident_sb[:, :], ident).then_inc(small_landed, 16)
            sp.wait_ge(tile_done, (CHUNKS - 1) * KT + 4)
            sp.dma_start(weight_f[:, :, :], weight).then_inc(weight_landed, 16)
            sp.wait_ge(spilled, 16 * SPILLED)
            sp.wait_ge(tile_done, (CHUNKS - 1) * KT + 6)
            sp.dma_start(h_all[:, 0, :, :], spill[0]).then_inc(reloaded[0], 16)
            for i in (1, 2):
                sp.wait_ge(quantised, FIRST if i == 1 else piece(1, 1) + 1)
                sp.dma_start(h_all[:, slot(i - 1), :, :], spill[i]).then_inc(reloaded[i], 16)

            sp.dma_start(x_last[:, :, :], x[ORDER[-1]]).then_inc(x_last_landed, 16)

            def store(m, b, i):
                for half in range(2):
                    ts = slice(half * KT // 2, (half + 1) * KT // 2)
                    sp.wait_ge(x_added[b][half], 16 * (m + 1))
                    sp.dma_start(out[i, :, ts, :], o[:, b, ts, :]).then_inc(o_free[b][half], 16)

            with sp.Fori(0, CHUNKS // 2 - 1) as m:
                for b in range(2):
                    store(m, b, 2 * m + b)
            store(CHUNKS // 2 - 1, 0, CHUNKS - 2)
            for t in range(KT):
                sp.wait_ge(last_out_ready, t + 1)
                sp.dma_start(out[CHUNKS - 1, :, t, :], o[:, 1, t, :]).then_inc(last_stored, 16)
            for b in range(2):
                for half in range(2):
                    sp.wait_ge(o_free[b][half], 16 * (CHUNKS // 2 + 1 - b))
            sp.wait_ge(last_stored, 16 * KT)

        @block.gpsimd
        def _(pool):
            nc.gpsimd.memset(xa[:, :, :].bitcast(f32), 0.0).then_inc(xa_zeroed, 1)

            def gather_a(c, pair, now):
                for one in range(2):
                    batch = c * PER_CHUNK + 2 * pair + one
                    n = pool.value_load(idx_i[0:1, bass.ds(batch, 1)], min_val=0, max_val=ADAPTERS - 1)
                    nc.gpsimd.tensor_copy(s_batch[:, bass.ds(batch, 1)], s_adapter[:, bass.ds(n, 1)])
                    done = nc.gpsimd.tensor_copy(now[:, :, one:one + 1, :], a_all[:, :, bass.ds(n, 1), :])
                done.then_inc(a_now_ready, 1)

            def gather_ahead(c):
                for pair in range(2):
                    pool.wait_ge(a_lo_ready, 2 * c + pair)
                    gather_a(c, pair, a_now)

            pool.wait_ge(idx_landed, 16)
            pool.wait_ge(scalings_landed, 16)
            pool.wait_ge(a_landed, 16)
            for pair in range(2):
                gather_a(0, pair, a_first[pair])
            with pool.Fori(0, SPILLED) as c:
                gather_ahead(c + 1)
                pool.wait_ge(banks_free, FIRST_CREDIT + (c + 1) * KT)
                pool.dma_start(spill[c], h_all[:, c + 1, :, :], max_dma_last_dim=16384).then_inc(spilled, 16)
                pool.wait_ge(spilled, 16 * (c + 1))
            with pool.Fori(SPILLED, CHUNKS - 1) as c:
                gather_ahead(c + 1)
            pool.wait_ge(x_lo_ready, CHUNKS * KT)
            nc.gpsimd.memset(ones[:, :], 1.0).then_inc(ones_ready, 1)
            for i in range(CHUNKS - 1):
                b = i % 2
                for half in range(2):
                    ts = slice(half * KT // 2, (half + 1) * KT // 2)
                    pool.wait_ge(banks_free, STAGE1 + i * KT + (half + 1) * KT // 2)
                    pool.dma_start(o[:, b, ts, :], x[ORDER[i], :, ts, :], accum_op=ALU.add,
                                   max_dma_last_dim=8192).then_inc(x_added[b][half], 16)

        @block.tensor
        def _(pe):
            def three(ps, hi, lo, mov_hi, mov_lo, start, stop):
                nc.tensor.matmul(ps, lo, mov_hi, start=start, stop=False)
                nc.tensor.matmul(ps, hi, mov_lo, start=False, stop=False)
                return nc.tensor.matmul(ps, hi, mov_hi, start=False, stop=stop)

            with pe.Fori(0, CHUNKS) as c:
                def w_times_x(t):
                    pe.wait_ge(w_lo_ready, t + 1)
                    if t != XA_BANK:
                        pe.wait_ge(banks_free, c * KT + t + 1)
                    for k in range(KT):
                        if t == 0:
                            pe.wait_ge(x_lo_ready, c * KT + k + 1)
                        last = three(bank[t][:, :], w_parts[t][:, 0, k, :], w_parts[t][:, 1, k, :],
                                     x_hi[:, k, :], x_lo[:, k, :], k == 0, False)
                        if t == KT - 1:
                            last.then_inc(x_used, 1)

                def a_times_x():
                    pe.wait_ge(banks_free, c * KT + XA_BANK + 1)
                    pe.wait_ge(a_lo_ready, 2 * (c + 1))
                    for k in range(KT):
                        hi, lo = (a_parts[:, part, k, :, :, :].rearrange("p j twice r -> p (j twice r)")
                                  for part in range(2))
                        last = three(bank[XA_BANK][:, :], hi, lo, x_hi[:, k, :], x_lo[:, k, :], k == 0, k == KT - 1)
                    last.then_inc(ax_done, 1)

                def b_times_ax(t):
                    for pair in range(2):
                        ns = slice(pair * 2 * SEQ, (pair + 1) * 2 * SEQ)
                        last = nc.tensor.matmul(bank[t][:, ns], b_parts[:, pair, t * P:(t + 1) * P],
                                                xa[:, pair, :], start=False, stop=pair == 1)
                    last.then_inc(tile_done, 1)

                w_times_x(0)
                a_times_x()
                w_times_x(1)
                pe.wait_ge(b_gathered, (c + 1) * 2 * PER_CHUNK * 16)
                pe.wait_ge(xa_lo_ready, (c + 1) * PER_CHUNK)
                b_times_ax(0)
                b_times_ax(1)
                for t in range(2, KT):
                    w_times_x(t)
                    b_times_ax(t)

            pe.wait_ge(small_landed, 16 * 2)
            pe.wait_ge(peak_ready, 1)
            for j in range(2):
                last = nc.tensor.matmul(bank[0][0:1, j * P:(j + 1) * P], peak[:, j:j + 1], ident_sb[:, :],
                                        start=True, stop=True)
            last.then_inc(peaks_turned, 1)
            pe.wait_ge(ones_ready, 1)
            pe.wait_ge(peak_row_ready, 1)
            nc.tensor.matmul(bank[1][:, 0:2], ones[0:1, :], peak_row[0:1, :],
                             start=True, stop=True).then_inc(peaks_spread, 1)

            for k in range(KT):
                pe.wait_ge(quantised, 2 * k + 2)
                for t in range(KT):
                    last = nc.tensor.matmul(bank[t][:, :], weight_q[:, k, t * P:(t + 1) * P], q[:, 0, k, :],
                                            start=k == 0, stop=k == KT - 1)
                    if k == KT - 1:
                        last.then_inc(tile2_done, 1)

            def chunk(i, b):
                for t in range(KT):
                    pe.wait_ge(banks_free, STAGE1 + (i - 1) * KT + t + 1)
                    for k in range(KT):
                        if t == 0 and k % (KT // 2) == 0:
                            pe.wait_ge(quantised, piece(i, k // (KT // 2)) + 1)
                        last = nc.tensor.matmul(bank[t][:, :], weight_q[:, k, t * P:(t + 1) * P], q[:, b, k, :],
                                                start=k == 0, stop=k == KT - 1)
                    last.then_inc(tile2_done, 1)

            chunk(1, 1)
            with pe.Fori(1, CHUNKS // 2) as m:
                chunk(2 * m, 0)
                chunk(2 * m + 1, 1)

        @block.scalar
        def _(act):
            def split_x(c, k):
                act.wait_ge(x_landed[k % LANDING], 16 * (2 * c + k // LANDING + 1))
                nc.scalar.activation(x_hi[:, k, :], x_land[:, k % LANDING, :], ACT.Copy).then_inc(x_hi_ready, 1)

            def split_w(t):
                act.wait_ge(w_landed[t], 16)
                nc.scalar.activation(w_parts[t][:, 0, :, :], w_land[:, t, :, :], ACT.Copy).then_inc(w_hi_ready, 1)

            def split_a(c, pair, now):
                act.wait_ge(a_now_ready, 2 * c + pair + 1)
                for twice in range(2):
                    done = nc.scalar.activation(a_parts[:, 0, :, 2 * pair:2 * pair + 2, twice, :], now[:, :, :, :],
                                                ACT.Copy)
                done.then_inc(a_hi_ready, 1)

            def chunk(c, s, first=False, last=False):
                act.wait_ge(ax_done, c + 1)
                for j in range(PER_CHUNK):
                    rows, _ = quadrants(j)
                    nc.scalar.activation(xa[rows, j // 2, (j % 2) * SEQ:(j % 2 + 1) * SEQ],
                                         bank[XA_BANK][rows, j * SEQ:(j + 1) * SEQ], ACT.Copy,
                                         scale=s_batch[rows, bass.ds(c * PER_CHUNK + j, 1)]
                                         ).then_inc(xa_hi_ready, 1)
                for t in range(KT):
                    if first and t + 2 < KT:
                        split_w(t + 2)
                    if not last and t in SPLIT_A:
                        split_a(c + 1, SPLIT_A.index(t), a_now)
                    if not last and t == KT - 1:
                        for k in range(KT):
                            act.wait_ge(x_used, c * KT + k + 1)
                            split_x(c + 1, k)
                    act.wait_ge(tile_done, c * KT + t + 1)
                    if last and t == KT - 1:
                        act.wait_ge(maxima_ready, CHUNKS * KT)
                    nc.scalar.activation(h_all[:, s, t, :], bank[t][:, :], ACT.Copy).then_inc(banks_free, 1)

            act.sem_inc(banks_free, FIRST_CREDIT)
            for b in range(2):
                for half in range(2):
                    act.sem_inc(o_free[b][half], 16)
            split_x(0, 0)
            split_w(0)
            for k in range(1, LANDING):
                split_x(0, k)
            act.wait_ge(b_landed, 16)
            nc.scalar.activation(b_hi[:, :].bitcast(f32r), b_land[:, :], ACT.Copy).then_inc(b_hi_ready, 1)
            for k in range(LANDING, KT):
                split_x(0, k)
            for pair in range(2):
                split_a(0, pair, a_first[pair])
            split_w(1)
            act.wait_ge(xa_zeroed, 1)
            act.wait_ge(b_table_ready, 32)
            chunk(0, slot(0), first=True)
            act.wait_ge(weight_maxima_ready, KT)
            act.wait_ge(w_lo_ready, KT)
            with act.Fori(1, SLOTS) as c:
                chunk(c, c + 1)
            with act.Fori(SLOTS, CHUNKS - 1) as c:
                act.wait_ge(spilled, 16 * (c - SLOTS + 1))
                chunk(c, c - SLOTS + 1)
            act.wait_ge(spilled, 16 * SPILLED)
            chunk(CHUNKS - 1, slot(CHUNKS - 1 - SLOTS), last=True)

            def magic_of(n, buffer, free, src, side, scaled=False):
                if free:
                    act.wait_ge(quantised, free)
                done = nc.scalar.activation(buffer, src, ACT.Abs, scale=inv_magic[:, side:side + 1])
                if scaled:
                    done = nc.scalar.activation(src, src, ACT.Copy, scale=inv[:, side:side + 1])
                done.then_inc(magic_raw, 1)

            def half_chunk(i, half, s, scaled=False):
                ks = slice(half * KT // 2, (half + 1) * KT // 2)
                n = piece(i, half)
                magic_of(n, half_magic(half), FIRST - 2 * (1 - half) if i == 1 else n - 1,
                         h_all[:, s, ks, :], 0, scaled)

            def evacuate(i, m, b, half):
                act.wait_ge(o_free[b][half], 16 * (m + 1))
                for t in range(half * KT // 2, (half + 1) * KT // 2):
                    act.wait_ge(tile2_done, i * KT + t + 1)
                    nc.scalar.activation(o[:, b, t, :], bank[t][:, :], ACT.Identity, bias=bias_sb[:, t:t + 1],
                                         scale=rescale[:, 0:1]).then_inc(banks_free, 1)

            act.wait_ge(scales_ready, 1)
            act.wait_ge(weight_landed, 16)
            for k in range(KT):
                for n, src in ((2 * k, h_all[:, slot(0), k, :]), (2 * k + 1, weight_f[:, k, :])):
                    magic_of(n, small_magic(n), max(0, n - SMALL_MAGICS + 1), src, n % 2, scaled=k > 0)
            half_chunk(1, 0, stage2_slot(1), scaled=True)
            half_chunk(1, 1, stage2_slot(1), scaled=True)
            act.wait_ge(rescale_ready, 1)
            evacuate(0, 0, 0, 0)
            half_chunk(2, 0, stage2_slot(2))
            evacuate(0, 0, 0, 1)
            for i in range(1, CHUNKS - 1):
                half_chunk(i + 1, 1, stage2_slot(i + 1))
                evacuate(i, i // 2, i % 2, 0)
                if i + 2 < CHUNKS:
                    if i + 2 >= SLOTS:
                        act.wait_ge(reloaded[i + 2 - SLOTS], 16)
                    half_chunk(i + 2, 0, stage2_slot(i + 2))
                evacuate(i, i // 2, i % 2, 1)
                if i == SLOTS:
                    act.wait_ge(x_last_landed, 16)
                    for t in range(KT):
                        nc.scalar.activation(x_last[:, t, :], x_last[:, t, :], ACT.Identity,
                                             bias=bias_sb[:, t:t + 1]).then_inc(x_last_ready, 1)

        @block.vector
        def _(dve):
            steps = [0]

            def then(instruction):
                steps[0] += 1
                instruction.then_inc(dve_step, 1)
                dve.wait_ge(dve_step, steps[0])

            def split_x(c, k):
                dve.wait_ge(x_hi_ready, c * KT + k + 1)
                nc.vector.tensor_tensor(x_lo[:, k, :], x_land[:, k % LANDING, :], x_hi[:, k, :].bitcast(f32),
                                        ALU.subtract).then_inc(x_lo_ready, 1)

            def split_w(t):
                dve.wait_ge(w_hi_ready, t + 1)
                nc.vector.tensor_tensor(w_parts[t][:, 1, :, :], w_land[:, t, :, :],
                                        w_parts[t][:, 0, :, :].bitcast(f32), ALU.subtract).then_inc(w_lo_ready, 1)

            def split_xa(c):
                for j in range(PER_CHUNK):
                    rows, low_rows = quadrants(j)
                    ns = slice((j % 2) * SEQ, (j % 2 + 1) * SEQ)
                    dve.wait_ge(xa_hi_ready, c * PER_CHUNK + j + 1)
                    nc.vector.scalar_tensor_tensor(xa[low_rows, j // 2, ns], bank[XA_BANK][rows, j * SEQ:(j + 1) * SEQ],
                                                   s_batch[rows, bass.ds(c * PER_CHUNK + j, 1)],
                                                   xa[rows, j // 2, ns].bitcast(f32),
                                                   ALU.mult, ALU.subtract).then_inc(xa_lo_ready, 1)

            def split_a(c, pair, now):
                dve.wait_ge(a_hi_ready, 2 * c + pair + 1)
                for twice in range(2):
                    done = nc.vector.tensor_tensor(a_parts[:, 1, :, 2 * pair:2 * pair + 2, twice, :], now[:, :, :, :],
                                                   a_parts[:, 0, :, 2 * pair:2 * pair + 2, twice, :].bitcast(f32),
                                                   ALU.subtract)
                done.then_inc(a_lo_ready, 1)

            def chunk(c, s, first=False, last=False):
                split_xa(c)
                for t in range(KT):
                    if first and t + 2 < KT:
                        split_w(t + 2)
                    if not last and t in SPLIT_A:
                        split_a(c + 1, SPLIT_A.index(t), a_now)
                    if not last and t == KT - 1:
                        for k in range(KT):
                            split_x(c + 1, k)
                    if last and t == KT - 1:
                        dve.wait_ge(tile_done, CHUNKS * KT)
                        h_tile = bank[t][:, :]
                    else:
                        dve.wait_ge(banks_free, FIRST_CREDIT + c * KT + t + 1)
                        h_tile = h_all[:, s, t, :]
                    nc.vector.tensor_reduce(maxima[:, bass.ds(c * KT + t, 1)], h_tile, AX.X, ALU.max,
                                            apply_absolute_value=True).then_inc(maxima_ready, 1)
                    if first and KT // 2 - 1 <= t < KT - 1:
                        dve.wait_ge(weight_early_landed, 16)
                        for k in (2 * t - KT + 2, 2 * t - KT + 3):
                            nc.vector.tensor_reduce(weight_maxima[:, k:k + 1], weight_early[:, k, :], AX.X, ALU.max,
                                                    apply_absolute_value=True).then_inc(weight_maxima_ready, 1)

            split_x(0, 0)
            split_w(0)
            for k in range(1, LANDING):
                split_x(0, k)
            dve.wait_ge(b_hi_ready, 1)
            nc.vector.tensor_tensor(b_lo[:, :].bitcast(f32r), b_land[:, :], b_hi[:, :],
                                    ALU.subtract).then_inc(b_lo_ready, 1)
            for k in range(LANDING, KT):
                split_x(0, k)
            for pair in range(2):
                split_a(0, pair, a_first[pair])
            split_w(1)
            chunk(0, slot(0), first=True)
            dve.wait_ge(weight_maxima_ready, KT)
            nc.vector.tensor_reduce(peak[:, 1:2], weight_maxima[:, :], AX.X, ALU.max)
            with dve.Fori(1, SLOTS) as c:
                chunk(c, c + 1)
            with dve.Fori(SLOTS, CHUNKS - 1) as c:
                chunk(c, c - SLOTS + 1)
            chunk(CHUNKS - 1, slot(CHUNKS - 1 - SLOTS), last=True)

            dve.wait_ge(maxima_ready, CHUNKS * KT)
            nc.vector.tensor_reduce(peak[:, 0:1], maxima[:, :], AX.X, ALU.max).then_inc(peak_ready, 1)
            dve.wait_ge(peaks_turned, 1)
            nc.vector.tensor_reduce(peak_row[0:1, :], bank[0][0:1, 0:2 * P].rearrange("a (j p) -> a j p", j=2),
                                    AX.X, ALU.max).then_inc(peak_row_ready, 1)
            dve.wait_ge(peaks_spread, 1)
            then(nc.vector.tensor_scalar(scale[:, :], bank[1][:, 0:2], 1.0 / FP8_RANGE, None, ALU.mult))
            then(nc.vector.tensor_tensor(scale[:, 1:2], scale[:, 0:1], scale[:, 1:2], ALU.max))
            then(nc.vector.reciprocal(inv[:, :], scale[:, :]))
            nc.vector.tensor_scalar(inv_magic[:, :], inv[:, :], TO_MAGIC, None, ALU.mult).then_inc(scales_ready, 1)
            nc.vector.tensor_tensor(rescale[:, :], scale[:, 0:1], scale[:, 1:2], ALU.mult).then_inc(rescale_ready, 1)

            def quantise(n, m, src, dst, side, scaled=False):
                dve.wait_ge(magic_raw, n + 1)
                if scaled:
                    nc.vector.scalar_tensor_tensor(src, m, MAGIC_FLOOR, src, ALU.max, ALU.add).then_inc(sum_ready, 1)
                    dve.wait_ge(sum_ready, n + 1)
                    nc.vector.scalar_tensor_tensor(dst, m, MAGIC_FLOOR, src,
                                                   ALU.max, ALU.subtract).then_inc(quantised, 1)
                    return
                nc.vector.tensor_scalar(m, m, MAGIC_FLOOR, None, ALU.max).then_inc(magic_ready, 1)
                dve.wait_ge(magic_ready, n + 1 - (SCALED if not isinstance(n, int) or n >= FIRST else 0))
                nc.vector.scalar_tensor_tensor(src, src, inv[:, side:side + 1], m,
                                               ALU.mult, ALU.add).then_inc(sum_ready, 1)
                dve.wait_ge(sum_ready, n + 1)
                nc.vector.tensor_tensor(dst, m, src, ALU.subtract).then_inc(quantised, 1)

            def quantise_chunk(i, b, s, scaled=False):
                for half in range(2):
                    ks = slice(half * KT // 2, (half + 1) * KT // 2)
                    quantise(piece(i, half), half_magic(half), h_all[:, s, ks, :], q[:, b, ks, :], 0, scaled)

            for k in range(KT):
                quantise(2 * k, small_magic(2 * k), h_all[:, slot(0), k, :], q[:, 0, k, :], 0, scaled=k > 0)
                quantise(2 * k + 1, small_magic(2 * k + 1), weight_f[:, k, :], weight_q[:, k, :], 1, scaled=k > 0)
            quantise_chunk(1, 1, stage2_slot(1), scaled=True)
            with dve.Fori(2, SLOTS) as i:
                dve.wait_ge(tile2_done, (i - 1) * KT)
                quantise_chunk(i, i % 2, i + 1)
            with dve.Fori(SLOTS, CHUNKS) as i:
                dve.wait_ge(tile2_done, (i - 1) * KT)
                quantise_chunk(i, i % 2, i - SLOTS)

            for t in range(KT):
                dve.wait_ge(x_last_ready, t + 1)
                dve.wait_ge(tile2_done, (CHUNKS - 1) * KT + t + 1)
                if t % (KT // 2) == 0:
                    dve.wait_ge(o_free[1][t // (KT // 2)], 16 * CHUNKS // 2)
                nc.vector.scalar_tensor_tensor(o[:, 1, t, :], bank[t][:, :], rescale[:, 0:1], x_last[:, t, :],
                                               ALU.mult, ALU.add).then_inc(last_out_ready, 1)


def kernel(x, itok_B_0_6, L0_cond_W, L0_cond_A, L0_cond_Bm, L0_cond_scalings, L0_ffn_weight, L0_ffn_bias):
    import numpy as np
    import concourse.bacc as bacc
    from concourse.bass_utils import run_bass_kernel_spmd

    def laid_out(a, *axes):
        return np.ascontiguousarray(np.transpose(a, axes))

    f = np.asarray
    arrays = {
        "x": laid_out(f(x).reshape(CHUNKS, N, KT, P), 0, 3, 2, 1),
        "idx": np.ascontiguousarray(np.broadcast_to(f(itok_B_0_6), (P, BATCH))),
        "W": laid_out(f(L0_cond_W).reshape(KT, P, KT, P), 3, 0, 2, 1),
        "A": laid_out(f(L0_cond_A).reshape(ADAPTERS, RANK, KT, P), 3, 2, 0, 1),
        "B": laid_out(f(L0_cond_Bm), 0, 2, 1).reshape(P, D),
        "scalings": np.ascontiguousarray(np.broadcast_to(f(L0_cond_scalings), (P, ADAPTERS))),
        "ident": np.eye(P, dtype=np.float32),
        "weight": laid_out(f(L0_ffn_weight).reshape(D, KT, P), 2, 1, 0),
        "bias": laid_out(f(L0_ffn_bias).reshape(KT, P), 1, 0),
    }
    nc = bacc.Bacc("TRN2", target_bir_lowering=False, num_devices=1)
    args = [nc.dram_tensor(f"in_{name}", a.shape, mybir.dt.from_np(a.dtype), kind="ExternalInput").ap()
            for name, a in arrays.items()]
    out = nc.dram_tensor("out", (CHUNKS, P, KT, N), mybir.dt.float32, kind="ExternalOutput").ap()
    adaln_ffn(nc, *args, out)
    run = run_bass_kernel_spmd(nc, [{f"in_{name}": a for name, a in arrays.items()}], core_ids=[0])
    got = np.empty((CHUNKS, N, KT, P), np.float32)
    got[ORDER] = run.results[0]["out"].transpose(0, 3, 2, 1)
    return got.reshape(BATCH, SEQ, D)
```

```python
import concourse.bass as bass
from concourse import mybir

P = 128
N = 512
CHUNKS = 8
D = 1024
KT = D // P
BATCH = 32
ADAPTERS = 8
RANK = 16
ROWS = 2 * RANK
SEQ = 128
PER_CHUNK = N // SEQ
SLOTS = 5
SPILLED = CHUNKS - SLOTS
LANDING = 4
BANKS = 8
SPLIT_A = [2, 3, 4, 5]
PEAK_FROM = 2
FIRST_CREDIT = BANKS
STAGE1 = FIRST_CREDIT + CHUNKS * KT
LAST_TILE = CHUNKS * KT - 1
FP8_RANGE = 448.0 * 0.8
TO_MAGIC = 2.0 ** 20
MAGIC_FLOOR = 1.5 * 2.0 ** 14
SMALL_MAGICS = 4
H_GUESSED = 4
GUESSED = KT + H_GUESSED
FIRST = KT - H_GUESSED
SCALED = 2
SIDE_BY_SIDE = 3
GUESS_BANK = 6
GUESS_AFTER = {-1: (0, 1), 2: (2, 3), 3: (4, 5), 4: (6, 7), 5: (8, 9, 10), 6: (11,)}
WEIGHT_LANDING = 5
ORDER = list(range(SLOTS, CHUNKS)) + list(range(SPILLED, SLOTS)) + list(range(SPILLED))


def piece(i, half):
    return FIRST + 2 * (i - 1) + half


def quadrants(j):
    low = (j + 2) % 4
    return slice(j * ROWS, (j + 1) * ROWS), slice(low * ROWS, (low + 1) * ROWS)


def adaln_ffn(nc, x, idx, W, A, B, scalings, pair_sum, ident, weight, bias, out):
    f32, f32r, bf16, i32 = mybir.dt.float32, mybir.dt.float32r, mybir.dt.bfloat16, mybir.dt.int32
    ALU, ACT, AX = mybir.AluOpType, mybir.ActivationFunctionType, mybir.AxisListType

    spill = nc.dram_tensor("spill", (SPILLED, P, KT, N), f32, kind="Internal").ap()
    b_table = nc.dram_tensor("b_table", (ADAPTERS, 2, RANK, D), f32, kind="Internal").ap()

    KiB = 1024
    base = (nc.sbuf_base + 63) // 64 * 64

    def at(name, kib, shape, dt):
        return nc.alloc_sbuf_tensor_at(name, shape, dt, offset=base + int(kib * KiB))

    W_PLACE = [0, 1, 2, 4, 6, 7, 3, 5]
    w_parts = [at(f"w_parts_{t}", 8 * W_PLACE[t], [P, 2, KT, P], f32r) for t in range(KT)]
    h_all = at("h_all", 48, [P, SLOTS + 1, KT, N], f32)
    x_hi = at("x_hi", 144, [P, KT, N], f32r)
    x_lo = at("x_lo", 160, [P, KT, N], f32r)
    a_all = at("a_all", 176, [P, KT, ADAPTERS, RANK], f32)
    a_parts = at("a_parts", 180, [P, KT, PER_CHUNK, 2, RANK], f32r)
    ax_hi = at("ax_hi", 184, [P, N], f32r)
    ax_lo = at("ax_lo", 186, [P, N], f32r)
    b_parts = at("b_parts", 188, [P, 2, D], f32r)
    xa = at("xa", 196, [P, 2, 2 * SEQ], f32r)
    x_land = at("x_land", 198, [P, LANDING, N], f32)
    b_land = at("b_land", 64, [P, D], f32)
    b_hi = at("b_hi", 68, [P, D], f32)
    b_lo = at("b_lo", 72, [P, D], f32)
    pair_sum_land = at("pair_sum_land", 78, [P, P], f32)
    x_first = at("x_first", 80, [P, KT - LANDING, N], f32)
    weight_early = at("weight_early", 80, [P, KT, D], f32)
    w_land = at("w_land", 112, [P, KT, KT, P], f32)
    weight_q = at("weight_q", 0, [P, KT, D], bf16)
    weight_land = [at(f"weight_land_{i}", kib, [P, D], f32)
                   for i, kib in enumerate((198, 202, 184, 16, 20))]
    h_scaled = at("h_scaled", 202, [P, 2, N], f32)
    weight_magic = at("weight_magic", 180, [P, 2, D], bf16)
    ident_sb = at("ident_sb", 176, [P, P], f32)
    ones = at("ones", 176.5, [1, P], f32)
    guess = at("guess", 177, [P, 2], f32)
    inv_guess = at("inv_guess", 177.03125, [P, 2], f32)
    inv_magic_guess = at("inv_magic_guess", 177.0625, [P, 2], f32)
    guessed_right = at("guessed_right", 177.09375, [P, 1], i32)
    q = at("q", 32, [P, 2, KT, N], bf16)
    o = at("o", 144, [P, 2, KT, N], f32)
    weight_f = at("weight_f", 144, [P, KT, D], f32)
    magic = at("magic", 192, [P, KT, N], bf16)
    x_last = at("x_last", 16, [P, KT, N], f32)
    SMALL = 206
    idx_i = at("idx_i", SMALL, [P, BATCH], i32)
    s_batch = at("s_batch", SMALL + 0.125, [P, BATCH], f32)
    s_adapter = at("s_adapter", SMALL + 0.25, [P, ADAPTERS], f32)
    weight_maxima = at("weight_maxima", SMALL + 0.28125, [P, KT], f32)
    maxima = at("maxima", SMALL + 0.3125, [P, CHUNKS * KT], f32)
    peak = at("peak", SMALL + 0.5625, [P, 2], f32)
    peak_row = at("peak_row", SMALL + 0.59375, [1, 2], f32)
    scale = at("scale", SMALL + 0.625, [P, 2], f32)
    inv = at("inv", SMALL + 0.65625, [P, 2], f32)
    inv_magic = at("inv_magic", SMALL + 0.6875, [P, 2], f32)
    rescale = at("rescale", SMALL + 0.71875, [P, 1], f32)
    bias_sb = at("bias_sb", SMALL + 0.75, [P, KT], f32)
    pair_sum_r = at("pair_sum_r", SMALL + 0.8125, [P, P], f32r)

    bank = [nc.alloc_psum_tensor(f"bank_{i}", [P, N], f32) for i in range(BANKS)]
    XA_BANK = BANKS - 1

    sem = nc.alloc_semaphore
    a_landed, b_landed, small_landed, scalings_landed = (
        sem("a_landed"), sem("b_landed"), sem("small_landed"), sem("scalings_landed"))
    w_landed = [sem(f"w_landed_{t}") for t in range(KT)]
    w0_landed = sem("w0_landed")
    weight_early_landed = [sem(f"weight_early_landed_{part}") for part in range(KT // 2)]
    weight_landed = sem("weight_landed")
    weight_land_landed = [sem(f"weight_land_landed_{i}") for i in range(WEIGHT_LANDING)]
    guess_ready, guess_raw, guess_sum, guess_quantised, guess_checked = (
        sem("guess_ready"), sem("guess_raw"), sem("guess_sum"), sem("guess_quantised"), sem("guess_checked"))
    again_inverse = sem("again_inverse")
    again_raw, again_sum, again_quantised, guessed_tiles_ready = (
        sem("again_raw"), sem("again_sum"), sem("again_quantised"), sem("guessed_tiles_ready"))
    x_landed = [sem(f"x_landed_{r}") for r in range(LANDING)]
    x_first_landed = [sem(f"x_first_landed_{r}") for r in range(KT - LANDING)]
    s_batch_ready, a_hi_ready, a_lo_ready = sem("s_batch_ready"), sem("a_hi_ready"), sem("a_lo_ready")
    b_hi_ready, b_lo_ready = sem("b_hi_ready"), sem("b_lo_ready")
    b_table_ready, b_gathered, xa_zeroed = sem("b_table_ready"), sem("b_gathered"), sem("xa_zeroed")
    idx_landed = sem("idx_landed")
    w_hi_ready, w_lo_ready = sem("w_hi_ready"), sem("w_lo_ready")
    x_hi_ready, x_lo_ready, x_used = sem("x_hi_ready"), sem("x_lo_ready"), sem("x_used")
    weight_maxima_ready = sem("weight_maxima_ready")
    pair_sum_landed, pair_sum_ready = sem("pair_sum_landed"), sem("pair_sum_ready")
    ax_done, ax_hi_ready, ax_lo_ready, ax_summed = (
        sem("ax_done"), sem("ax_hi_ready"), sem("ax_lo_ready"), sem("ax_summed"))
    xa_hi_ready, xa_lo_ready = sem("xa_hi_ready"), sem("xa_lo_ready")
    x_last_landed, x_last_ready, last_out_ready, last_stored = (
        sem("x_last_landed"), sem("x_last_ready"), sem("last_out_ready"), sem("last_stored"))
    tile_done, banks_free, maxima_ready = sem("tile_done"), sem("banks_free"), sem("maxima_ready")
    spilled = sem("spilled")
    ones_ready, peak_ready, peaks_turned, peak_row_ready = (
        sem("ones_ready"), sem("peak_ready"), sem("peaks_turned"), sem("peak_row_ready"))
    peaks_spread, dve_step, scales_ready, rescale_ready = (
        sem("peaks_spread"), sem("dve_step"), sem("scales_ready"), sem("rescale_ready"))
    reloaded = [sem(f"reloaded_{c}") for c in range(SPILLED)]
    magic_raw, magic_ready, sum_ready, quantised = (
        sem("magic_raw"), sem("magic_ready"), sem("sum_ready"), sem("quantised"))
    tile2_done = sem("tile2_done")
    x_added = [[sem(f"x_added_{b}{half}") for half in range(2)] for b in range(2)]
    o_free = [[sem(f"o_free_{b}{half}") for half in range(2)] for b in range(2)]

    def x_landing(c, k):
        if isinstance(c, int) and c == 0:
            if k < LANDING:
                return x_land[:, k, :], x_landed[k], 16
            return x_first[:, k - LANDING, :], x_first_landed[k - LANDING], 16
        return x_land[:, k % LANDING, :], x_landed[k % LANDING], 16 * (2 * c + k // LANDING)

    def w_pieces(t):
        half = KT // 2
        return [(slice(0, half), w0_landed, 1), (slice(half, KT), w_landed[0], 2)] if t == 0 else [
            (slice(0, KT), w_landed[t], t + 2)]

    def adapter(engine, c, j):
        return engine.value_load(idx_i[0:1, bass.ds(c * PER_CHUNK + j, 1)], min_val=0, max_val=ADAPTERS - 1)

    def a_of(n):
        return a_all[:, :, bass.ds(n, 1), :].rearrange("p k one r -> p k (one r)")

    def slot(s):
        return s + 1

    def stage2_slot(i):
        return i + 1 if i < SLOTS else i - SLOTS

    def half_magic(half):
        return magic[:, half * 4:(half + 1) * 4, :]

    def small_magic(n):
        return magic[:, 2 * (SMALL_MAGICS - FIRST + n), :]

    def guess_piece(n, again=False):
        if n < KT:
            source = weight_f[:, n, :] if again else weight_land[n % WEIGHT_LANDING][:, :]
            return source, source, weight_q[:, n, :], 1
        k = n - KT
        source = h_all[:, slot(0), k, :]
        return source, h_scaled[:, n % 2, :], q[:, 0, k, :], 0

    def guess_magic(n):
        return weight_magic[:, n % 2, :] if n < KT else weight_magic[:, n % 2, 0:N]

    with nc.Block() as block:

        @block.sync
        def _(sp):
            def load_x(c, k):
                land, landed, _ = x_landing(c, k)
                sp.dma_start(land, x[c, :, k, :]).then_inc(landed, 16)

            def load_w(t):
                for ks, landed, _ in w_pieces(t):
                    sp.dma_start(w_land[:, t, ks, :], W[:, t, ks, :]).then_inc(landed, 16)

            def gather_b(c):
                for j in range(PER_CHUNK):
                    n = sp.value_load(idx_i[0:1, bass.ds(c * PER_CHUNK + j, 1)], min_val=0, max_val=ADAPTERS - 1)
                    for rows in quadrants(j):
                        sp.dma_start(b_parts[rows, j // 2, :].bitcast(f32),
                                     b_table[n, :, :, :].rearrange("part r o -> (part r) o")
                                     ).then_inc(b_gathered, 16)

            load_x(0, 0)
            load_w(0)
            for k in range(1, LANDING):
                load_x(0, k)
            sp.dma_start(idx_i[:, :], idx).then_inc(idx_landed, 16)
            sp.dma_start(a_all[:, :, :, :], A).then_inc(a_landed, 16)
            for k in range(LANDING, KT):
                load_x(0, k)
            load_w(1)
            sp.dma_start(s_adapter[:, :], scalings).then_inc(scalings_landed, 16)
            sp.dma_start(pair_sum_land[:, :], pair_sum).then_inc(pair_sum_landed, 16)
            sp.dma_start(b_land[:, :], B).then_inc(b_landed, 16)
            load_w(2)
            load_w(3)
            sp.wait_ge(b_hi_ready, 1)
            sp.dma_start(b_table[:, 0, :, :], b_hi[:, :]).then_inc(b_table_ready, 16)
            sp.wait_ge(b_lo_ready, 1)
            sp.dma_start(b_table[:, 1, :, :], b_lo[:, :]).then_inc(b_table_ready, 16)
            sp.wait_ge(b_table_ready, 32)
            gather_b(0)
            for t in range(4, KT):
                load_w(t)
            sp.wait_ge(x_lo_ready, KT)
            for part in range(KT // 2):
                sp.dma_start(weight_early[:, 2 * part:2 * part + 2, :],
                             weight[:, 2 * part:2 * part + 2, :]).then_inc(weight_early_landed[part], 16)
            sp.dma_start(bias_sb[:, :], bias).then_inc(small_landed, 16)
            with sp.Fori(1, CHUNKS) as c:
                for k in range(KT):
                    sp.wait_ge(x_lo_ready, c * KT + k - LANDING + 1)
                    load_x(c, k)
                sp.wait_ge(tile_done, c * KT)
                gather_b(c)
            sp.wait_ge(a_lo_ready, CHUNKS * PER_CHUNK)
            sp.dma_start(ident_sb[:, :], ident).then_inc(small_landed, 16)
            for k in range(KT):
                if k == 0:
                    sp.wait_ge(x_lo_ready, CHUNKS * KT)
                if k == 2:
                    sp.wait_ge(ax_summed, CHUNKS)
                if k == 3:
                    sp.wait_ge(tile_done, (CHUNKS - 1) * KT + 3)
                if k >= WEIGHT_LANDING:
                    sp.wait_ge(guess_quantised, k - WEIGHT_LANDING + 1)
                sp.dma_start(weight_land[k % WEIGHT_LANDING][:, :],
                             weight[:, k, :]).then_inc(weight_land_landed[k % WEIGHT_LANDING], 16)
            sp.wait_ge(spilled, 16 * SPILLED)
            sp.wait_ge(tile_done, (CHUNKS - 1) * KT + 6)
            sp.dma_start(h_all[:, 0, :, :], spill[0]).then_inc(reloaded[0], 16)
            sp.wait_ge(guess_checked, 1)
            right = sp.value_load(guessed_right[0:1, 0:1], min_val=0, max_val=1)
            with sp.If(right == 0):
                sp.dma_start(weight_f[:, :, :], weight).then_inc(weight_landed, 16)
            for i in (1, 2):
                sp.wait_ge(quantised, FIRST if i == 1 else piece(1, 1) + 1)
                sp.dma_start(h_all[:, slot(i - 1), :, :], spill[i]).then_inc(reloaded[i], 16)
            sp.dma_start(x_last[:, :, :], x[ORDER[-1]]).then_inc(x_last_landed, 16)

            def store(m, b, i):
                for half in range(2):
                    ts = slice(half * KT // 2, (half + 1) * KT // 2)
                    sp.wait_ge(x_added[b][half], 16 * (m + 1))
                    sp.dma_start(out[i, :, ts, :], o[:, b, ts, :]).then_inc(o_free[b][half], 16)

            with sp.Fori(0, CHUNKS // 2 - 1) as m:
                for b in range(2):
                    store(m, b, 2 * m + b)
            store(CHUNKS // 2 - 1, 0, CHUNKS - 2)
            for t in range(KT):
                sp.wait_ge(last_out_ready, t + 1)
                sp.dma_start(out[CHUNKS - 1, :, t, :], o[:, 1, t, :]).then_inc(last_stored, 16)
            for b in range(2):
                for half in range(2):
                    sp.wait_ge(o_free[b][half], 16 * (CHUNKS // 2 + 1 - b))
            sp.wait_ge(last_stored, 16 * KT)

        @block.gpsimd
        def _(pool):
            nc.gpsimd.memset(xa[:, :, :].bitcast(f32), 0.0).then_inc(xa_zeroed, 1)

            pool.wait_ge(idx_landed, 16)
            pool.wait_ge(scalings_landed, 16)
            with pool.Fori(0, BATCH) as batch:
                n = pool.value_load(idx_i[0:1, bass.ds(batch, 1)], min_val=0, max_val=ADAPTERS - 1)
                nc.gpsimd.tensor_copy(s_batch[:, bass.ds(batch, 1)],
                                      s_adapter[:, bass.ds(n, 1)]).then_inc(s_batch_ready, 1)
            with pool.Fori(0, SPILLED) as c:
                pool.wait_ge(banks_free, FIRST_CREDIT + (c + 1) * KT)
                pool.dma_start(spill[c], h_all[:, c + 1, :, :], max_dma_last_dim=16384).then_inc(spilled, 16)
                pool.wait_ge(spilled, 16 * (c + 1))
            pool.wait_ge(a_lo_ready, CHUNKS * PER_CHUNK)
            nc.gpsimd.memset(ones[:, :], 1.0).then_inc(ones_ready, 1)
            for i in range(CHUNKS - 1):
                b = i % 2
                for half in range(2):
                    ts = slice(half * KT // 2, (half + 1) * KT // 2)
                    pool.wait_ge(banks_free, STAGE1 + i * KT + (half + 1) * KT // 2)
                    pool.dma_start(o[:, b, ts, :], x[ORDER[i], :, ts, :], accum_op=ALU.add,
                                   max_dma_last_dim=8192).then_inc(x_added[b][half], 16)

        @block.tensor
        def _(pe):
            def three(ps, hi, lo, mov_hi, mov_lo, start, stop):
                nc.tensor.matmul(ps, lo, mov_hi, start=start, stop=False)
                nc.tensor.matmul(ps, hi, mov_lo, start=False, stop=False)
                return nc.tensor.matmul(ps, hi, mov_hi, start=False, stop=stop)

            def peaks_of_all(n, columns, turned, spread):
                def turn():
                    pe.wait_ge(small_landed, 16 * 2)
                    pe.wait_ge(peak_ready, n)
                    for j, column in enumerate(columns):
                        last = nc.tensor.matmul(turned[0:1, j * P:(j + 1) * P], column, ident_sb[:, :],
                                                start=True, stop=True)
                    last.then_inc(peaks_turned, 1)

                def spread_out():
                    pe.wait_ge(ones_ready, 1)
                    pe.wait_ge(peak_row_ready, n)
                    nc.tensor.matmul(spread, ones[0:1, :], peak_row[0:1, :],
                                     start=True, stop=True).then_inc(peaks_spread, 1)
                return turn, spread_out

            def stage1_chunk(c, last_chunk=False):
                def w_times_x(t):
                    pe.wait_ge(w_lo_ready, w_pieces(t)[0][2])
                    if t != XA_BANK:
                        pe.wait_ge(banks_free, c * KT + t + 1)
                    for k in range(KT):
                        if t == 0 and k == KT // 2:
                            pe.wait_ge(w_lo_ready, w_pieces(0)[1][2])
                        if t == 0:
                            pe.wait_ge(x_lo_ready, c * KT + k + 1)
                        last = three(bank[t][:, :], w_parts[t][:, 0, k, :], w_parts[t][:, 1, k, :],
                                     x_hi[:, k, :], x_lo[:, k, :], k == 0, False)
                        if t == KT - 1:
                            last.then_inc(x_used, 1)

                def a_times_x():
                    pe.wait_ge(banks_free, c * KT + XA_BANK + 1)
                    pe.wait_ge(a_lo_ready, (c + 1) * PER_CHUNK)
                    for k in range(KT):
                        a_k = a_parts[:, k, :, :, :].rearrange("p j part r -> p (j part r)")
                        nc.tensor.matmul(bank[XA_BANK][:, :], a_k, x_lo[:, k, :], start=k == 0, stop=False)
                        last = nc.tensor.matmul(bank[XA_BANK][:, :], a_k, x_hi[:, k, :], start=False, stop=k == KT - 1)
                    last.then_inc(ax_done, 1)

                def sum_ax_pairs():
                    pe.wait_ge(pair_sum_ready, 1)
                    pe.wait_ge(ax_lo_ready, c + 1)
                    nc.tensor.matmul(bank[XA_BANK][:, :], pair_sum_r[:, :], ax_lo[:, :], start=True, stop=False)
                    nc.tensor.matmul(bank[XA_BANK][:, :], pair_sum_r[:, :], ax_hi[:, :],
                                     start=False, stop=True).then_inc(ax_summed, 1)

                def b_times_ax(t):
                    for pair in range(2):
                        ns = slice(pair * 2 * SEQ, (pair + 1) * 2 * SEQ)
                        last = nc.tensor.matmul(bank[t][:, ns], b_parts[:, pair, t * P:(t + 1) * P],
                                                xa[:, pair, :], start=False, stop=pair == 1)
                    last.then_inc(tile_done, 1)

                w_times_x(0)
                a_times_x()
                if last_chunk:
                    turn, spread_out = peaks_of_all(1, (peak[:, 0:1], peak[:, 1:2]), bank[GUESS_BANK][:, :],
                                                     bank[GUESS_BANK][:, 2 * P:2 * P + 2])
                    pe.wait_ge(banks_free, c * KT + GUESS_BANK + 1)
                    turn()
                w_times_x(1)
                if last_chunk:
                    spread_out()
                sum_ax_pairs()
                w_times_x(2)
                pe.wait_ge(b_gathered, (c + 1) * 2 * PER_CHUNK * 16)
                pe.wait_ge(xa_lo_ready, (c + 1) * PER_CHUNK)
                for t in range(3):
                    b_times_ax(t)
                for t in range(3, KT):
                    if last_chunk and t == GUESS_BANK:
                        pe.wait_ge(guess_ready, 1)
                    w_times_x(t)
                    b_times_ax(t)

            with pe.Fori(0, CHUNKS - 1) as c:
                stage1_chunk(c)
            stage1_chunk(CHUNKS - 1, last_chunk=True)

            turn, spread_out = peaks_of_all(2, (peak[:, 0:1], maxima[:, LAST_TILE:LAST_TILE + 1]), bank[0][:, :],
                                             bank[1][:, 0:2])
            pe.wait_ge(maxima_ready, CHUNKS * KT)
            turn()
            spread_out()

            def product2(t, b, k):
                return nc.tensor.matmul(bank[t][:, :], weight_q[:, k, t * P:(t + 1) * P], q[:, b, k, :],
                                        start=k == 0, stop=k == KT - 1)

            pe.wait_ge(guessed_tiles_ready, 1)
            for k in range(SIDE_BY_SIDE):
                for t in range(KT):
                    if k == 0:
                        pe.wait_ge(banks_free, STAGE1 - KT + t + 1)
                    product2(t, 0, k)
            for t in range(KT):
                for k in range(SIDE_BY_SIDE, KT):
                    if t == 0 and k >= H_GUESSED:
                        pe.wait_ge(quantised, k - H_GUESSED + 1)
                    last = product2(t, 0, k)
                last.then_inc(tile2_done, 1)

            def chunk(i, b):
                for t in range(KT):
                    pe.wait_ge(banks_free, STAGE1 + (i - 1) * KT + t + 1)
                    for k in range(KT):
                        if t == 0 and k % (KT // 2) == 0:
                            pe.wait_ge(quantised, piece(i, k // (KT // 2)) + 1)
                        last = product2(t, b, k)
                    last.then_inc(tile2_done, 1)

            chunk(1, 1)
            with pe.Fori(1, CHUNKS // 2) as m:
                chunk(2 * m, 0)
                chunk(2 * m + 1, 1)

        @block.scalar
        def _(act):
            def split_x(c, k):
                land, landed, count = x_landing(c, k)
                act.wait_ge(landed, count)
                nc.scalar.activation(x_hi[:, k, :], land, ACT.Copy).then_inc(x_hi_ready, 1)

            def split_w(t):
                for ks, landed, _ in w_pieces(t):
                    act.wait_ge(landed, 16)
                    nc.scalar.activation(w_parts[t][:, 0, ks, :], w_land[:, t, ks, :], ACT.Copy).then_inc(w_hi_ready, 1)

            def split_a(j, n):
                nc.scalar.activation(a_parts[:, :, j, 0, :], a_of(n), ACT.Copy).then_inc(a_hi_ready, 1)

            def magic_on_guess(n):
                if n == 0:
                    act.wait_ge(guess_ready, 1)
                if n < KT:
                    act.wait_ge(weight_land_landed[n % WEIGHT_LANDING], 16 * (n // WEIGHT_LANDING + 1))
                if n >= 2:
                    act.wait_ge(guess_quantised, n - 1)
                source, scaled, _, side = guess_piece(n)
                nc.scalar.activation(guess_magic(n), source, ACT.Abs, scale=inv_magic_guess[:, side:side + 1])
                nc.scalar.activation(scaled, source, ACT.Copy, scale=inv_guess[:, side:side + 1]).then_inc(guess_raw, 1)

            def chunk(c, s, first=False, last=False):
                act.wait_ge(ax_done, c + 1)
                nc.scalar.activation(ax_hi[:, :], bank[XA_BANK][:, :], ACT.Copy).then_inc(ax_hi_ready, 1)
                act.wait_ge(s_batch_ready, (c + 1) * PER_CHUNK)
                act.wait_ge(ax_summed, c + 1)
                for j in range(PER_CHUNK):
                    rows, _ = quadrants(j)
                    nc.scalar.activation(xa[rows, j // 2, (j % 2) * SEQ:(j % 2 + 1) * SEQ],
                                         bank[XA_BANK][rows, j * SEQ:(j + 1) * SEQ], ACT.Copy,
                                         scale=s_batch[rows, bass.ds(c * PER_CHUNK + j, 1)]
                                         ).then_inc(xa_hi_ready, 1)
                if last:
                    for n in GUESS_AFTER[-1]:
                        magic_on_guess(n)
                for t in range(KT):
                    if first and t + 3 < KT:
                        split_w(t + 3)
                    if not last and t in SPLIT_A:
                        split_a(SPLIT_A.index(t), adapter(act, c + 1, SPLIT_A.index(t)))
                    if not last and t == KT - 1:
                        for k in range(KT):
                            act.wait_ge(x_used, c * KT + k + 1)
                            split_x(c + 1, k)
                    act.wait_ge(tile_done, c * KT + t + 1)
                    if last and t == KT - 1:
                        act.wait_ge(maxima_ready, CHUNKS * KT)
                    nc.scalar.activation(h_all[:, s, t, :], bank[t][:, :], ACT.Copy).then_inc(banks_free, 1)
                    if last:
                        for n in GUESS_AFTER.get(t, ()):
                            magic_on_guess(n)

            act.sem_inc(banks_free, FIRST_CREDIT)
            for b in range(2):
                for half in range(2):
                    act.sem_inc(o_free[b][half], 16)
            split_x(0, 0)
            split_w(0)
            for k in range(1, LANDING):
                split_x(0, k)
            act.wait_ge(idx_landed, 16)
            first_adapters = [adapter(act, 0, j) for j in range(PER_CHUNK)]
            act.wait_ge(a_landed, 16)
            for j, n in enumerate(first_adapters):
                split_a(j, n)
            for k in range(LANDING, KT):
                split_x(0, k)
            split_w(1)
            act.wait_ge(b_landed, 16)
            nc.scalar.activation(b_hi[:, :].bitcast(f32r), b_land[:, :], ACT.Copy).then_inc(b_hi_ready, 1)
            split_w(2)
            act.wait_ge(pair_sum_landed, 16)
            nc.scalar.activation(pair_sum_r[:, :], pair_sum_land[:, :], ACT.Copy).then_inc(pair_sum_ready, 1)
            act.wait_ge(xa_zeroed, 1)
            act.wait_ge(b_table_ready, 32)
            chunk(0, slot(0), first=True)
            act.wait_ge(weight_maxima_ready, KT)
            act.wait_ge(w_lo_ready, KT + 1)
            with act.Fori(1, SLOTS) as c:
                chunk(c, c + 1)
            with act.Fori(SLOTS, CHUNKS - 1) as c:
                act.wait_ge(spilled, 16 * (c - SLOTS + 1))
                chunk(c, c - SLOTS + 1)
            act.wait_ge(spilled, 16 * SPILLED)
            chunk(CHUNKS - 1, slot(CHUNKS - 1 - SLOTS), last=True)

            def magic_of(n, buffer, free, src, side, scaled=False):
                if free:
                    act.wait_ge(quantised, free)
                done = nc.scalar.activation(buffer, src, ACT.Abs, scale=inv_magic[:, side:side + 1])
                if scaled:
                    done = nc.scalar.activation(src, src, ACT.Copy, scale=inv[:, side:side + 1])
                done.then_inc(magic_raw, 1)

            def half_chunk(i, half, s, scaled=False):
                ks = slice(half * KT // 2, (half + 1) * KT // 2)
                n = piece(i, half)
                magic_of(n, half_magic(half), FIRST - 2 * (1 - half) if i == 1 else n - 1,
                         h_all[:, s, ks, :], 0, scaled)

            def evacuate(i, m, b, half):
                act.wait_ge(o_free[b][half], 16 * (m + 1))
                for t in range(half * KT // 2, (half + 1) * KT // 2):
                    act.wait_ge(tile2_done, i * KT + t + 1)
                    nc.scalar.activation(o[:, b, t, :], bank[t][:, :], ACT.Identity, bias=bias_sb[:, t:t + 1],
                                         scale=rescale[:, 0:1]).then_inc(banks_free, 1)

            def magic_once_more():
                act.wait_ge(weight_landed, 16)
                act.wait_ge(again_inverse, 2)
                for n in range(GUESSED):
                    if n >= 2:
                        act.wait_ge(again_quantised, n - 1)
                    source, scaled, _, side = guess_piece(n, again=True)
                    nc.scalar.activation(guess_magic(n), source, ACT.Abs, scale=inv_magic[:, side:side + 1])
                    nc.scalar.activation(scaled, source, ACT.Copy, scale=inv[:, side:side + 1]).then_inc(again_raw, 1)

            act.wait_ge(scales_ready, 1)
            for n in range(FIRST):
                magic_of(n, small_magic(n), 0, h_all[:, slot(0), H_GUESSED + n, :], 0)
            act.wait_ge(guess_checked, 1)
            right = act.value_load(guessed_right[0:1, 0:1], min_val=0, max_val=1)
            with act.If(right == 0):
                magic_once_more()
            half_chunk(1, 0, stage2_slot(1), scaled=True)
            half_chunk(1, 1, stage2_slot(1), scaled=True)
            act.wait_ge(rescale_ready, 1)
            evacuate(0, 0, 0, 0)
            half_chunk(2, 0, stage2_slot(2))
            evacuate(0, 0, 0, 1)
            for i in range(1, CHUNKS - 1):
                half_chunk(i + 1, 1, stage2_slot(i + 1))
                evacuate(i, i // 2, i % 2, 0)
                if i + 2 < CHUNKS:
                    if i + 2 >= SLOTS:
                        act.wait_ge(reloaded[i + 2 - SLOTS], 16)
                    half_chunk(i + 2, 0, stage2_slot(i + 2))
                evacuate(i, i // 2, i % 2, 1)
                if i == SLOTS:
                    act.wait_ge(x_last_landed, 16)
                    for t in range(KT):
                        nc.scalar.activation(x_last[:, t, :], x_last[:, t, :], ACT.Identity,
                                             bias=bias_sb[:, t:t + 1]).then_inc(x_last_ready, 1)

        @block.vector
        def _(dve):
            steps = [0]

            def then(*instructions):
                for instruction in instructions:
                    steps[0] += 1
                    instruction.then_inc(dve_step, 1)
                dve.wait_ge(dve_step, steps[0])

            def split_x(c, k):
                dve.wait_ge(x_hi_ready, c * KT + k + 1)
                land, _, _ = x_landing(c, k)
                nc.vector.tensor_tensor(x_lo[:, k, :], land, x_hi[:, k, :].bitcast(f32),
                                        ALU.subtract).then_inc(x_lo_ready, 1)

            def split_w(t):
                for ks, _, count in w_pieces(t):
                    dve.wait_ge(w_hi_ready, count)
                    nc.vector.tensor_tensor(w_parts[t][:, 1, ks, :], w_land[:, t, ks, :],
                                            w_parts[t][:, 0, ks, :].bitcast(f32), ALU.subtract).then_inc(w_lo_ready, 1)

            def split_xa(c):
                for j in range(PER_CHUNK):
                    rows, low_rows = quadrants(j)
                    ns = slice((j % 2) * SEQ, (j % 2 + 1) * SEQ)
                    dve.wait_ge(xa_hi_ready, c * PER_CHUNK + j + 1)
                    nc.vector.scalar_tensor_tensor(xa[low_rows, j // 2, ns], bank[XA_BANK][rows, j * SEQ:(j + 1) * SEQ],
                                                   s_batch[rows, bass.ds(c * PER_CHUNK + j, 1)],
                                                   xa[rows, j // 2, ns].bitcast(f32),
                                                   ALU.mult, ALU.subtract).then_inc(xa_lo_ready, 1)

            def split_a(c, j, n):
                dve.wait_ge(a_hi_ready, c * PER_CHUNK + j + 1)
                nc.vector.tensor_tensor(a_parts[:, :, j, 1, :], a_of(n), a_parts[:, :, j, 0, :].bitcast(f32),
                                        ALU.subtract).then_inc(a_lo_ready, 1)

            def step_on_guess(n, raw, summed, done, again=False):
                _, v, to, _ = guess_piece(n, again)
                dve.wait_ge(raw, n + 1)
                nc.vector.scalar_tensor_tensor(v, guess_magic(n), MAGIC_FLOOR, v, ALU.max, ALU.add).then_inc(summed, 1)
                dve.wait_ge(summed, n + 1)
                nc.vector.scalar_tensor_tensor(to, guess_magic(n), MAGIC_FLOOR, v,
                                               ALU.max, ALU.subtract).then_inc(done, 1)

            def peak_of(tiles):
                dve.wait_ge(maxima_ready, tiles)
                return nc.vector.tensor_reduce(peak[:, 0:1], maxima[:, 0:tiles], AX.X, ALU.max)

            def guess_scale():
                dve.wait_ge(peaks_turned, 1)
                nc.vector.tensor_reduce(peak_row[0:1, :],
                                        bank[GUESS_BANK][0:1, 0:2 * P].rearrange("a (j p) -> a j p", j=2),
                                        AX.X, ALU.max).then_inc(peak_row_ready, 1)
                dve.wait_ge(peaks_spread, 1)
                then(nc.vector.tensor_scalar(guess[:, :], bank[GUESS_BANK][:, 2 * P:2 * P + 2],
                                             1.0 / FP8_RANGE, None, ALU.mult))
                then(nc.vector.tensor_tensor(guess[:, 1:2], guess[:, 0:1], guess[:, 1:2], ALU.max))
                then(nc.vector.reciprocal(inv_guess[:, :], guess[:, :]))
                nc.vector.tensor_scalar(inv_magic_guess[:, :], inv_guess[:, :], TO_MAGIC, None,
                                        ALU.mult).then_inc(guess_ready, 1)

            def chunk(c, s, first=False, last=False):
                if last:
                    peak_of((CHUNKS - 1) * KT).then_inc(peak_ready, 1)
                dve.wait_ge(ax_hi_ready, c + 1)
                nc.vector.tensor_tensor(ax_lo[:, :], bank[XA_BANK][:, :], ax_hi[:, :].bitcast(f32),
                                        ALU.subtract).then_inc(ax_lo_ready, 1)
                if last:
                    guess_scale()
                dve.wait_ge(s_batch_ready, (c + 1) * PER_CHUNK)
                split_xa(c)
                if last:
                    for n in GUESS_AFTER[-1]:
                        step_on_guess(n, guess_raw, guess_sum, guess_quantised)
                for t in range(KT):
                    if first and t + 3 < KT:
                        split_w(t + 3)
                    if not last and t in SPLIT_A:
                        split_a(c + 1, SPLIT_A.index(t), adapter(dve, c + 1, SPLIT_A.index(t)))
                    if not last and t == KT - 1:
                        for k in range(KT):
                            split_x(c + 1, k)
                    if last and t == KT - 1:
                        peak_of(LAST_TILE).then_inc(peak_ready, 1)
                        dve.wait_ge(tile_done, CHUNKS * KT)
                        h_tile = bank[t][:, :]
                    else:
                        dve.wait_ge(banks_free, FIRST_CREDIT + c * KT + t + 1)
                        h_tile = h_all[:, s, t, :]
                    nc.vector.tensor_reduce(maxima[:, bass.ds(c * KT + t, 1)], h_tile, AX.X, ALU.max,
                                            apply_absolute_value=True).then_inc(maxima_ready, 1)
                    if last:
                        for n in GUESS_AFTER.get(t, ()):
                            step_on_guess(n, guess_raw, guess_sum, guess_quantised)
                    if first and 0 <= t - PEAK_FROM < KT // 2:
                        dve.wait_ge(weight_early_landed[t - PEAK_FROM], 16)
                        for k in (2 * (t - PEAK_FROM), 2 * (t - PEAK_FROM) + 1):
                            nc.vector.tensor_reduce(weight_maxima[:, k:k + 1], weight_early[:, k, :], AX.X, ALU.max,
                                                    apply_absolute_value=True).then_inc(weight_maxima_ready, 1)

            split_x(0, 0)
            split_w(0)
            for k in range(1, LANDING):
                split_x(0, k)
            dve.wait_ge(idx_landed, 16)
            first_adapters = [adapter(dve, 0, j) for j in range(PER_CHUNK)]
            dve.wait_ge(a_landed, 16)
            for j, n in enumerate(first_adapters):
                split_a(0, j, n)
            for k in range(LANDING, KT):
                split_x(0, k)
            split_w(1)
            dve.wait_ge(b_hi_ready, 1)
            nc.vector.tensor_tensor(b_lo[:, :].bitcast(f32r), b_land[:, :], b_hi[:, :],
                                    ALU.subtract).then_inc(b_lo_ready, 1)
            split_w(2)
            chunk(0, slot(0), first=True)
            dve.wait_ge(weight_maxima_ready, KT)
            nc.vector.tensor_reduce(peak[:, 1:2], weight_maxima[:, :], AX.X, ALU.max)
            with dve.Fori(1, SLOTS) as c:
                chunk(c, c + 1)
            with dve.Fori(SLOTS, CHUNKS - 1) as c:
                chunk(c, c - SLOTS + 1)
            chunk(CHUNKS - 1, slot(CHUNKS - 1 - SLOTS), last=True)

            dve.wait_ge(peaks_turned, 2)
            nc.vector.tensor_reduce(peak_row[0:1, 0:1], bank[0][0:1, 0:2 * P],
                                    AX.X, ALU.max).then_inc(peak_row_ready, 1)
            dve.wait_ge(peaks_spread, 2)
            then(nc.vector.tensor_scalar(scale[:, :], bank[1][:, 0:2], 1.0 / FP8_RANGE, None, ALU.mult))
            nc.vector.tensor_tensor(guessed_right[:, :], scale[:, 0:1], guess[:, 0:1],
                                    ALU.is_equal).then_inc(guess_checked, 1)
            then(nc.vector.reciprocal(inv[:, 0:1], scale[:, 0:1]),
                 nc.vector.tensor_tensor(scale[:, 1:2], scale[:, 0:1], scale[:, 1:2], ALU.max))
            nc.vector.tensor_scalar(inv_magic[:, 0:1], inv[:, 0:1], TO_MAGIC, None, ALU.mult).then_inc(scales_ready, 1)
            nc.vector.tensor_tensor(rescale[:, :], scale[:, 0:1], scale[:, 1:2], ALU.mult).then_inc(rescale_ready, 1)

            dve.wait_ge(guess_checked, 1)
            right = dve.value_load(guessed_right[0:1, 0:1], min_val=0, max_val=1)
            with dve.If(right == 0):
                nc.vector.reciprocal(inv[:, 1:2], scale[:, 1:2]).then_inc(again_inverse, 1)
                dve.wait_ge(again_inverse, 1)
                nc.vector.tensor_scalar(inv_magic[:, 1:2], inv[:, 1:2], TO_MAGIC, None,
                                        ALU.mult).then_inc(again_inverse, 1)
                for n in range(GUESSED):
                    step_on_guess(n, again_raw, again_sum, again_quantised, again=True)
                dve.wait_ge(again_quantised, GUESSED)
            dve.wait_ge(guess_quantised, GUESSED)
            dve.sem_inc(guessed_tiles_ready, 1)

            def quantise(n, m, src, dst, side, scaled=False):
                dve.wait_ge(magic_raw, n + 1)
                if scaled:
                    nc.vector.scalar_tensor_tensor(src, m, MAGIC_FLOOR, src, ALU.max, ALU.add).then_inc(sum_ready, 1)
                    dve.wait_ge(sum_ready, n + 1)
                    nc.vector.scalar_tensor_tensor(dst, m, MAGIC_FLOOR, src,
                                                   ALU.max, ALU.subtract).then_inc(quantised, 1)
                    return
                nc.vector.tensor_scalar(m, m, MAGIC_FLOOR, None, ALU.max).then_inc(magic_ready, 1)
                dve.wait_ge(magic_ready, n + 1 if isinstance(n, int) and n < FIRST else n + 1 - SCALED)
                nc.vector.scalar_tensor_tensor(src, src, inv[:, side:side + 1], m,
                                               ALU.mult, ALU.add).then_inc(sum_ready, 1)
                dve.wait_ge(sum_ready, n + 1)
                nc.vector.tensor_tensor(dst, m, src, ALU.subtract).then_inc(quantised, 1)

            def quantise_chunk(i, b, s, scaled=False):
                for half in range(2):
                    ks = slice(half * KT // 2, (half + 1) * KT // 2)
                    quantise(piece(i, half), half_magic(half), h_all[:, s, ks, :], q[:, b, ks, :], 0, scaled)

            for n in range(FIRST):
                k = H_GUESSED + n
                quantise(n, small_magic(n), h_all[:, slot(0), k, :], q[:, 0, k, :], 0)
            quantise_chunk(1, 1, stage2_slot(1), scaled=True)
            with dve.Fori(2, SLOTS) as i:
                dve.wait_ge(tile2_done, (i - 1) * KT)
                quantise_chunk(i, i % 2, i + 1)
            with dve.Fori(SLOTS, CHUNKS) as i:
                dve.wait_ge(tile2_done, (i - 1) * KT)
                quantise_chunk(i, i % 2, i - SLOTS)

            for t in range(KT):
                dve.wait_ge(x_last_ready, t + 1)
                dve.wait_ge(tile2_done, (CHUNKS - 1) * KT + t + 1)
                if t % (KT // 2) == 0:
                    dve.wait_ge(o_free[1][t // (KT // 2)], 16 * CHUNKS // 2)
                nc.vector.scalar_tensor_tensor(o[:, 1, t, :], bank[t][:, :], rescale[:, 0:1], x_last[:, t, :],
                                               ALU.mult, ALU.add).then_inc(last_out_ready, 1)


def kernel(x, itok_B_0_6, L0_cond_W, L0_cond_A, L0_cond_Bm, L0_cond_scalings, L0_ffn_weight, L0_ffn_bias):
    import numpy as np
    import concourse.bacc as bacc
    from concourse.bass_utils import run_bass_kernel_spmd

    def laid_out(a, *axes):
        return np.ascontiguousarray(np.transpose(a, axes))

    f = np.asarray
    arrays = {
        "x": laid_out(f(x).reshape(CHUNKS, N, KT, P), 0, 3, 2, 1),
        "idx": np.ascontiguousarray(np.broadcast_to(f(itok_B_0_6), (P, BATCH))),
        "W": laid_out(f(L0_cond_W).reshape(KT, P, KT, P), 3, 0, 2, 1),
        "A": laid_out(f(L0_cond_A).reshape(ADAPTERS, RANK, KT, P), 3, 2, 0, 1),
        "B": laid_out(f(L0_cond_Bm), 0, 2, 1).reshape(P, D),
        "scalings": np.ascontiguousarray(np.broadcast_to(f(L0_cond_scalings), (P, ADAPTERS))),
        "pair_sum": np.kron(np.kron(np.eye(PER_CHUNK), np.ones((2, 2))), np.eye(RANK)).astype(np.float32),
        "ident": np.eye(P, dtype=np.float32),
        "weight": laid_out(f(L0_ffn_weight).reshape(D, KT, P), 2, 1, 0),
        "bias": laid_out(f(L0_ffn_bias).reshape(KT, P), 1, 0),
    }
    nc = bacc.Bacc("TRN2", target_bir_lowering=False, num_devices=1)
    args = [nc.dram_tensor(f"in_{name}", a.shape, mybir.dt.from_np(a.dtype), kind="ExternalInput").ap()
            for name, a in arrays.items()]
    out = nc.dram_tensor("out", (CHUNKS, P, KT, N), mybir.dt.float32, kind="ExternalOutput").ap()
    adaln_ffn(nc, *args, out)
    run = run_bass_kernel_spmd(nc, [{f"in_{name}": a for name, a in arrays.items()}], core_ids=[0])
    got = np.empty((CHUNKS, N, KT, P), np.float32)
    got[ORDER] = run.results[0]["out"].transpose(0, 3, 2, 1)
    return got.reshape(BATCH, SEQ, D)
```
